# Optimizing a Trainium2 kernel written in Bass

```python
import numpy as np
import jax
import jax.numpy as jnp

def _softmax(x, axis=-1):
    return jax.nn.softmax(x, axis=axis)

def _gelu(x):
    return jax.nn.gelu(x, approximate=True)

def _silu(x):
    return jax.nn.silu(x)

def _sigmoid(x):
    return jax.nn.sigmoid(x)

def _layernorm(x, axis=-1, eps=1e-05):
    m = jnp.mean(x, axis=axis, keepdims=True)
    v = jnp.var(x, axis=axis, keepdims=True)
    return (x - m) / jnp.sqrt(v + eps)

def _scatter_add(tgt, idx, src, axis=0):
    return tgt.at[idx].add(src)

def _segment_sum(src, seg, n):
    return jax.ops.segment_sum(src, seg, n)
kernel_name = 'mk_early_fusion_d1_tok_img1024_r4_737e49'

def setup_inputs(seed: int=0):
    np.random.seed(seed)
    _w = jnp.asarray

    def _rec_inputs():
        import jax
        import jax.numpy as jnp
        _rk = jax.random.key(seed)
        x = -0.00016672 + 0.999947 * jax.random.normal(jax.random.fold_in(_rk, 1), (64, 3, 96, 96), jnp.float32)
        txt = -6.04713e-11 + 0.999984 * jax.random.normal(jax.random.fold_in(_rk, 2), (64, 128, 256), jnp.float32)
        return (x, txt)
    x, txt = _rec_inputs()

    def _L0_tok_setup():
        import jax, jax.numpy as jnp
        import numpy as np
        PATCH = 16
        EPS = 1e-05

        def _patchify(x, p):
            B, C, H, W = x.shape
            hp, wp = (H // p, W // p)
            x = x.reshape(B, C, hp, p, wp, p)
            x = x.transpose(0, 2, 4, 1, 3, 5)
            return x.reshape(B, hp * wp, C * p * p)
        key = jax.random.key(seed)
        ks = jax.random.split(key, 6)
        B, C, H = (64, 3, 96)
        E = 256
        P = PATCH
        N = (H // P) ** 2
        D = C * P * P
        x = jax.random.normal(ks[0], (B, C, H, H), dtype=jnp.float32)
        W = jax.random.normal(ks[1], (D, E), dtype=jnp.float32) * (1.0 / np.sqrt(D))
        b = jnp.zeros((E,), dtype=jnp.float32)
        cls_token = jax.random.normal(ks[2], (1, 1, E), dtype=jnp.float32) * 0.02
        pos_embedding = jax.random.normal(ks[3], (1, N + 1, E), dtype=jnp.float32) * 0.02
        gamma = jnp.ones((E,), dtype=jnp.float32)
        beta = jnp.zeros((E,), dtype=jnp.float32)
        return {'x': x, 'W': W, 'b': b, 'cls_token': cls_token, 'pos_embedding': pos_embedding, 'gamma': gamma, 'beta': beta}
    _L0_tok_all = _L0_tok_setup()
    _L0_tok_in = {k: v for k, v in _L0_tok_all.items() if k in ('W', 'b', 'cls_token', 'pos_embedding', 'gamma', 'beta')}
    del _L0_tok_all

    def _L0_attn_setup():
        import jax, jax.numpy as jnp
        import numpy as np
        B, T, D, H = (2, 512, 256, 16)
        key = jax.random.key(seed)
        ks = jax.random.split(key, 5)
        s = 0.02
        return {'x': jax.random.normal(ks[0], (B, T, D), dtype=jnp.float32), 'W_qkv': jax.random.normal(ks[1], (3 * D, D), dtype=jnp.float32) * s, 'b_qkv': jnp.zeros((3 * D,), dtype=jnp.float32), 'W_out': jax.random.normal(ks[2], (D, D), dtype=jnp.float32) * s, 'b_out': jnp.zeros((D,), dtype=jnp.float32)}
    _L0_attn_all = _L0_attn_setup()
    _L0_attn_in = {k: v for k, v in _L0_attn_all.items() if k in ('W_qkv', 'b_qkv', 'W_out', 'b_out')}
    del _L0_attn_all

    def _L0_ffn_setup():
        import jax, jax.numpy as jnp
        import numpy as np
        B, S, D = (1, 512, 256)
        E, K, F = (64, 8, 192)
        SF = 192
        C = 128
        ROUTED_SCALE = 1.0

        def _moe_forward(x, router_w, w_gate, w_up, w_down, ws_gate_up, ws_down):
            T = x.shape[0]
            logits = x.astype(jnp.float32) @ router_w.T
            probs = jax.nn.softmax(logits, axis=-1)
            topk_w, topk_ids = jax.lax.top_k(probs, K)
            topk_w = topk_w / jnp.sum(topk_w, axis=-1, keepdims=True)
            topk_w = topk_w.astype(x.dtype)
            N = T * K
            flat_e = topk_ids.reshape(-1)
            flat_w = topk_w.reshape(-1)
            tok = jnp.arange(N) // K
            onehot = flat_e[:, None] == jnp.arange(E)[None, :]
            pos = jnp.cumsum(onehot, axis=0)[jnp.arange(N), flat_e] - 1
            valid = pos < C
            idx = jnp.where(valid, flat_e * C + pos, E * C)
            x_buf = jnp.zeros((E * C + 1, x.shape[1]), x.dtype).at[idx].set(x[tok])
            xb = x_buf[:E * C].reshape(E, C, -1)
            g = jnp.einsum('ecd,edf->ecf', xb, w_gate)
            u = jnp.einsum('ecd,edf->ecf', xb, w_up)
            h = jax.nn.silu(g) * u
            y = jnp.einsum('ecf,efd->ecd', h, w_down).reshape(E * C, -1)
            safe = jnp.where(valid, idx, 0)
            contrib = y[safe] * (flat_w * valid.astype(flat_w.dtype))[:, None]
            routed = jax.ops.segment_sum(contrib, tok, num_segments=T)
            routed = routed * ROUTED_SCALE
            gu = x @ ws_gate_up
            sg, su = (gu[:, :SF], gu[:, SF:])
            shared = jax.nn.silu(sg) * su @ ws_down
            return routed + shared
        key = jax.random.key(seed)
        ks = jax.random.split(key, 7)
        w = 0.02
        return {'hidden_states': jax.random.normal(ks[0], (B, S, D), jnp.float32), 'router_w': jax.random.normal(ks[1], (E, D), jnp.float32) * w, 'w_gate': jax.random.normal(ks[2], (E, D, F), jnp.float32) * w, 'w_up': jax.random.normal(ks[3], (E, D, F), jnp.float32) * w, 'w_down': jax.random.normal(ks[4], (E, F, D), jnp.float32) * w, 'ws_gate_up': jax.random.normal(ks[5], (D, 2 * SF), jnp.float32) * w, 'ws_down': jax.random.normal(ks[6], (SF, D), jnp.float32) * w}
    _L0_ffn_all = _L0_ffn_setup()
    _L0_ffn_in = {k: v for k, v in _L0_ffn_all.items() if k in ('router_w', 'w_gate', 'w_up', 'w_down', 'ws_gate_up', 'ws_down')}
    del _L0_ffn_all
    return {'x': x, 'txt': txt, 'L0_tok_W': _L0_tok_in['W'], 'L0_tok_b': _L0_tok_in['b'], 'L0_tok_cls_token': _L0_tok_in['cls_token'], 'L0_tok_pos_embedding': _L0_tok_in['pos_embedding'], 'L0_tok_gamma': _L0_tok_in['gamma'], 'L0_tok_beta': _L0_tok_in['beta'], 'L0_attn_W_qkv': _L0_attn_in['W_qkv'], 'L0_attn_b_qkv': _L0_attn_in['b_qkv'], 'L0_attn_W_out': _L0_attn_in['W_out'], 'L0_attn_b_out': _L0_attn_in['b_out'], 'L0_ffn_router_w': _L0_ffn_in['router_w'], 'L0_ffn_w_gate': _L0_ffn_in['w_gate'], 'L0_ffn_w_up': _L0_ffn_in['w_up'], 'L0_ffn_w_down': _L0_ffn_in['w_down'], 'L0_ffn_ws_gate_up': _L0_ffn_in['ws_gate_up'], 'L0_ffn_ws_down': _L0_ffn_in['ws_down']}

def reference(x, txt, L0_tok_W, L0_tok_b, L0_tok_cls_token, L0_tok_pos_embedding, L0_tok_gamma, L0_tok_beta, L0_attn_W_qkv, L0_attn_b_qkv, L0_attn_W_out, L0_attn_b_out, L0_ffn_router_w, L0_ffn_w_gate, L0_ffn_w_up, L0_ffn_w_down, L0_ffn_ws_gate_up, L0_ffn_ws_down):
    import jax
    import jax.numpy as jnp

    def _L0_tok_ref(x, W, b, cls_token, pos_embedding, gamma, beta):
        import jax, jax.numpy as jnp
        import numpy as np
        PATCH = 16
        EPS = 1e-05

        def _patchify(x, p):
            B, C, H, W = x.shape
            hp, wp = (H // p, W // p)
            x = x.reshape(B, C, hp, p, wp, p)
            x = x.transpose(0, 2, 4, 1, 3, 5)
            return x.reshape(B, hp * wp, C * p * p)
        B = x.shape[0]
        patches = _patchify(x, PATCH)
        tok = jnp.einsum('bnd,de->bne', patches, W) + b
        cls = jnp.broadcast_to(cls_token, (B, 1, tok.shape[-1]))
        h = jnp.concatenate([cls, tok], axis=1) + pos_embedding
        mu = jnp.mean(h, axis=-1, keepdims=True)
        var = jnp.mean(jnp.square(h - mu), axis=-1, keepdims=True)
        out = (h - mu) * jax.lax.rsqrt(var + EPS) * gamma + beta
        return out

    def _L0_attn_ref(x, W_qkv, b_qkv, W_out, b_out):
        import jax, jax.numpy as jnp
        import numpy as np
        B, T, D, H = (2, 512, 256, 16)
        Bx, Tx, Dx = x.shape
        Hh = H
        hd = Dx // Hh
        topk = max(1, int(Tx * 0.3))
        scale = Dx ** (-0.5)
        qkv = x @ W_qkv.T + b_qkv
        qkv = qkv.reshape(Bx, Tx, 3, Hh, hd)
        q = jnp.transpose(qkv[:, :, 0], (0, 2, 1, 3))
        k = jnp.transpose(qkv[:, :, 1], (0, 2, 1, 3))
        v = jnp.transpose(qkv[:, :, 2], (0, 2, 1, 3))
        scores = jnp.einsum('bhid,bhjd->bhij', q, k) * scale
        topk_scores, indices = jax.lax.top_k(scores, topk)
        bi = jnp.arange(Bx)[:, None, None, None]
        hi = jnp.arange(Hh)[None, :, None, None]
        ti = jnp.arange(Tx)[None, None, :, None]
        masked = jnp.full_like(scores, -jnp.inf)
        masked = masked.at[bi, hi, ti, indices].set(topk_scores)
        attn = jax.nn.softmax(masked, axis=-1)
        out = jnp.einsum('bhij,bhjd->bhid', attn, v)
        out = jnp.transpose(out, (0, 2, 1, 3)).reshape(Bx, Tx, Dx)
        return out @ W_out.T + b_out

    def _L0_ffn_ref(hidden_states, router_w, w_gate, w_up, w_down, ws_gate_up, ws_down):
        import jax, jax.numpy as jnp
        import numpy as np
        B, S, D = (1, 512, 256)
        E, K, F = (64, 8, 192)
        SF = 192
        C = 128
        ROUTED_SCALE = 1.0

        def _moe_forward(x, router_w, w_gate, w_up, w_down, ws_gate_up, ws_down):
            T = x.shape[0]
            logits = x.astype(jnp.float32) @ router_w.T
            probs = jax.nn.softmax(logits, axis=-1)
            topk_w, topk_ids = jax.lax.top_k(probs, K)
            topk_w = topk_w / jnp.sum(topk_w, axis=-1, keepdims=True)
            topk_w = topk_w.astype(x.dtype)
            N = T * K
            flat_e = topk_ids.reshape(-1)
            flat_w = topk_w.reshape(-1)
            tok = jnp.arange(N) // K
            onehot = flat_e[:, None] == jnp.arange(E)[None, :]
            pos = jnp.cumsum(onehot, axis=0)[jnp.arange(N), flat_e] - 1
            valid = pos < C
            idx = jnp.where(valid, flat_e * C + pos, E * C)
            x_buf = jnp.zeros((E * C + 1, x.shape[1]), x.dtype).at[idx].set(x[tok])
            xb = x_buf[:E * C].reshape(E, C, -1)
            g = jnp.einsum('ecd,edf->ecf', xb, w_gate)
            u = jnp.einsum('ecd,edf->ecf', xb, w_up)
            h = jax.nn.silu(g) * u
            y = jnp.einsum('ecf,efd->ecd', h, w_down).reshape(E * C, -1)
            safe = jnp.where(valid, idx, 0)
            contrib = y[safe] * (flat_w * valid.astype(flat_w.dtype))[:, None]
            routed = jax.ops.segment_sum(contrib, tok, num_segments=T)
            routed = routed * ROUTED_SCALE
            gu = x @ ws_gate_up
            sg, su = (gu[:, :SF], gu[:, SF:])
            shared = jax.nn.silu(sg) * su @ ws_down
            return routed + shared
        b, s, d = hidden_states.shape
        x = hidden_states.reshape(-1, d)
        out = _moe_forward(x, router_w, w_gate, w_up, w_down, ws_gate_up, ws_down)
        return out.reshape(b, s, d)
    h = _L0_tok_ref(x, L0_tok_W, L0_tok_b, L0_tok_cls_token, L0_tok_pos_embedding, L0_tok_gamma, L0_tok_beta)
    h = jnp.concatenate([h, txt], axis=1)
    h = h + _L0_attn_ref(_layernorm(h, axis=-1), L0_attn_W_qkv, L0_attn_b_qkv, L0_attn_W_out, L0_attn_b_out)
    h = h + _L0_ffn_ref(_layernorm(h, axis=-1), L0_ffn_router_w, L0_ffn_w_gate, L0_ffn_w_up, L0_ffn_w_down, L0_ffn_ws_gate_up, L0_ffn_ws_down)
    return h

_drawn_inputs = setup_inputs


def setup_inputs(seed=0):
    import zlib

    import numpy as np

    out = dict(_drawn_inputs(seed))
    spreads = {'L0_tok_b': (0.0, 0.1),
     'L0_tok_gamma': (1.0, 0.2),
     'L0_tok_beta': (0.0, 0.1),
     'L0_attn_b_qkv': (0.0, 0.1),
     'L0_attn_b_out': (0.0, 0.1)}
    factors = {'L0_attn_W_qkv': 3.343,
     'L0_ffn_router_w': 8.0,
     'L0_ffn_w_gate': 8.0,
     'L0_ffn_w_up': 8.0,
     'L0_ffn_w_down': 8.0,
     'L0_ffn_ws_gate_up': 3.908,
     'L0_ffn_ws_down': 3.932}
    for name, (base, spread) in spreads.items():
        noise = np.random.default_rng([zlib.crc32(name.encode()), seed]).standard_normal(out[name].shape)
        drawn = base * np.exp(spread * noise) if base else spread * noise
        out[name] = jnp.asarray(drawn.astype(out[name].dtype))
    for name, factor in factors.items():
        out[name] = (out[name] * factor).astype(out[name].dtype)
    return out
```

```python
import concourse.bass as bass
from concourse import mybir
from contextlib import ExitStack

fp32 = mybir.dt.float32
i32 = mybir.dt.int32
u32 = mybir.dt.uint32
ALU = mybir.AluOpType
ACT = mybir.ActivationFunctionType
AX = mybir.AxisListType

P = 128
D = 256
KC = D // P
IMG = 37
TXT = 128
T = IMG + TXT
PK = 768 // P
NH = 16
HD = D // NH
HALF = NH // 2
ROWS = NH * T
NT = -(-ROWS // P)
HROWS = HALF * T
MIXED = HROWS // P
LEAD = HROWS - MIXED * P
QW = (MIXED + 1) * P
GROUP = 3
NG = NT // GROUP
TOPK = int(T * 0.3)
ROUNDS = TOPK // 8
NE = 64
FF = 192
FC = 96
NF = FF // FC
CAP = 128
SLOTS = NE * CAP
FAR = 2 * SLOTS
XW = D + NE
RING = 4
FIRST = 3
EB = 4
EPS = 1e-5
SCALE = float(D) ** -0.5
LOW = -3.0e38
GONE = -1.0e38
assert TOPK == 8 * ROUNDS + 1 and NT % GROUP == 0


def early_fusion_kernel(nc, patches, txt, w_tok, b_tok, cls, pos, gamma, beta, w_qkv, b_q, b_k, b_v, w_out, b_out,
                        router, w_gate, w_up, w_down, ws_gate_up, ws_down, out, n_batch):
    tokens = n_batch * T
    ctx = ExitStack()
    with ctx:
        def sb(name, shape, dt=fp32):
            return ctx.enter_context(nc.sbuf_tensor(name, shape, dt))

        def sem(name):
            return ctx.enter_context(nc.semaphore(name))

        x_rows = nc.dram_tensor("x_rows", (tokens + CAP, XW), fp32).ap()
        slot_token = nc.dram_tensor("slot_token", (SLOTS, 1), i32).ap()

        WT = sb("WT", [P, PK, D])
        WQ = sb("WQ", [P, KC, 3 * D])
        WO = sb("WO", [P, KC, D])
        WR = sb("WR", [P, KC, NE])
        WSG = sb("WSG", [P, KC, 2 * FF])
        WSD = sb("WSD", [FC, NF, D])
        POSB = sb("POSB", [IMG, D])
        BT = sb("BT", [IMG, D])
        GAM = sb("GAM", [IMG, D])
        BET = sb("BET", [IMG, D])
        BQ = sb("BQ", [P, KC])
        BK = sb("BK", [P, KC])
        BV = sb("BV", [P, KC])
        BVR = sb("BVR", [P, KC, P])
        BO = sb("BO", [P, D])
        IDENT = sb("IDENT", [P, P])
        TRI = sb("TRI", [P, P])
        ONES = sb("ONES", [P, P])
        ONESZ = sb("ONESZ", [P, 2, 2 * HD])
        PAD = sb("PAD", [P, 2, NE])
        CST = sb("CST", [P, NE])
        PW = sb("PW", [P, 2])
        ZR = sb("ZR", [P, XW])
        PT = [sb(f"PT{n}", [P, PK, IMG]) for n in range(2)]
        H = [sb(f"H{n}", [P, 2, D]) for n in range(RING)]
        TK = sb("TK", [IMG, D])
        st = sb("st", [P, 2, 6])
        mv = sb("mv", [P, 2, 2])
        ve = sb("ve", [P, 2])
        rs = sb("rs", [P, 2])
        XN = sb("XN", [P, 2, D])
        XT = sb("XT", [P, KC, T])
        QT = sb("QT", [P, KC, T])
        KT = sb("KT", [P, KC, T])
        ks = sb("ks", [P, KC])
        KZ = sb("KZ", [P, KC, T])
        QA = sb("QA", [P, QW])
        QB = sb("QB", [P, QW])
        VZ = [sb(f"VZ{n}", [P, 2, NH * 2 * HD]) for n in range(RING)]
        S = [sb(f"S{n}", [P, NT, T]) for n in range(2)]
        E = [sb(f"E{n}", [P, NT, T]) for n in range(2)]
        mx = sb("mx", [P, NT])
        nb = sb("nb", [P, NT])
        M8 = sb("M8", [P, NT, 8])
        LT = sb("LT", [P, NT, 8])
        PTT = sb("PTT", [P, NT * P])
        PTI = sb("PTI", [P, NT * P])
        RD = sb("RD", [P, KC, T])
        CT = sb("CT", [P, KC, T])
        HM = sb("HM", [P, 2, D])
        bst = sb("bst", [P, 2, 6])
        bmv = sb("bmv", [P, 2, 2])
        bve = sb("bve", [P, 2])
        brs = sb("brs", [P, 2])
        X2 = [sb(f"X2{n}", [P, 2, XW]) for n in range(2)]
        X2T = sb("X2T", [P, KC, T])
        TH = sb("TH", [FC, NF, T])
        HT = sb("HT", [FC, NF, T])
        OT = [sb(f"OT{n}", [P, 2, D]) for n in range(2)]
        L8 = sb("L8", [P, 2, 8])
        nl = sb("nl", [P, 2])
        MR = sb("MR", [P, 2, NE])
        MK = sb("MK", [P, 2, NE])
        EX = sb("EX", [P, 2, NE])
        e8 = sb("e8", [P, 2, 8])
        s8 = sb("s8", [P, 2])
        r8 = sb("r8", [P, 2])
        PO = sb("PO", [P, 2, NE])
        KEEP = sb("KEEP", [P, 2, NE])
        carry = sb("carry", [P, NE])
        N8 = sb("N8", [P, 2, 8])
        SLOT = [sb(f"SLOT{n}", [P, 2, 8], u32) for n in range(2)]
        tokf = sb("tokf", [P, 2])
        TOKI = [sb(f"TOKI{n}", [P, 2], i32) for n in range(2)]

        ids_i = sb("ids_i", [NE, CAP], i32)
        ids_f = sb("ids_f", [NE, CAP])
        ids_t = sb("ids_t", [CAP, NE], u32)
        IX = [sb(f"IX{n}", [CAP, 1], u32) for n in range(EB)]
        XG = [sb(f"XG{n}", [CAP, XW]) for n in range(EB)]
        Y = [sb(f"Y{n}", [CAP, D]) for n in range(EB)]
        WG = [sb(f"WG{n}", [P, KC, FF]) for n in range(EB)]
        WU = [sb(f"WU{n}", [P, KC, FF]) for n in range(EB)]
        WD = [sb(f"WD{n}", [FC, NF, D]) for n in range(EB)]
        XE = sb("XE", [P, KC, CAP])
        TE = sb("TE", [FC, NF, CAP])
        TG = sb("TG", [FC, NF, CAP])
        HE = sb("HE", [FC, NF, CAP])

        banks = [ctx.enter_context(nc.psum_tensor(f"bank{n}", [P, 512], fp32)) for n in range(8)]
        bS, bT, bI, bF, bX, bY = banks[0:3], banks[3], banks[4], banks[5], banks[6], banks[7]

        def chunks(bank, n, w):
            return bank[:, 0:n * w].rearrange("p (c n) -> p c n", c=n)

        s_const, s_wts, s_setup = sem("s_const"), sem("s_wts"), sem("s_setup")
        s_bo, s_z, s_bv = sem("s_bo"), sem("s_z"), sem("s_bv")
        s_patch, s_txt = [sem(f"s_patch{n}") for n in range(2)], [sem(f"s_txt{n}") for n in range(RING)]
        s_fp, FP = sem("s_fp"), 5
        s_fd, FD = sem("s_fd"), 9
        s_fa, FA = sem("s_fa"), 6
        s_fg, FG = sem("s_fg"), 10
        s_diag, DG = sem("s_diag"), 16 * NH
        s_score = sem("s_score")
        s_take = sem("s_take")
        s_exp, EX_N = sem("s_exp"), NG + NT
        s_top, TOP_N = sem("s_top"), (2 * ROUNDS + 2) * NT + 1
        s_prob = sem("s_prob")
        s_tr, TR_N = sem("s_tr"), NT
        s_trc, TRC_N = sem("s_trc"), 2 * -(-NT // 4)
        s_bp, BP = sem("s_bp"), 9
        s_bd, BD = sem("s_bd"), 28
        s_ba, BA = sem("s_ba"), 7
        s_bg, BG = sem("s_bg"), 4
        s_xrow, s_out = [[sem(f"{what}{n}") for n in range(2)] for what in ("s_xrow", "s_out")]
        s_slot, SL = [sem(f"s_slot{n}") for n in range(2)], 16 * 16
        s_zero, s_empty = sem("s_zero"), sem("s_empty")
        s_gate_d, s_gate_g, s_gate_s = sem("s_gate_d"), sem("s_gate_g"), sem("s_gate_s")
        s_ids, s_idt, s_idp = sem("s_ids"), sem("s_idt"), sem("s_idp")
        s_ew, s_xg = [[sem(f"{what}{n}") for n in range(EB)] for what in ("s_ew", "s_xg")]
        s_ix, s_ep, s_ea, s_ed, s_add = sem("s_ix"), sem("s_ep"), sem("s_ea"), sem("s_ed"), sem("s_add")

        block = ctx.enter_context(nc.Block())

        def batches(eng, body):
            loops = max(0, (n_batch - 2 - FIRST) // RING)
            for i in range(-1, FIRST):
                body(i, i % RING)
            if loops > 1:
                with eng.Fori(0, loops) as n:
                    for u in range(RING):
                        body(n * RING + FIRST + u, (FIRST + u) % RING)
            else:
                loops = 0
            for i in range(FIRST + RING * loops, n_batch + 2):
                body(i, i % RING)

        def experts(eng, body):
            for k in range(EB):
                body(k, k)
            with eng.Fori(1, NE // EB - 1) as n:
                for k in range(EB):
                    body(n * EB + k, k)
            for k in range(EB):
                body(NE - EB + k, k)

        def stored(eng):
            eng.wait_ge(s_zero, 32)
            for s in s_xrow, s_out:
                for n in range(2):
                    eng.wait_ge(s[n], 32 * len(range(n, n_batch, 2)))

        def of_ring(b, r, ring, n):
            return (n // ring) * (b - r) + n

        def known(i):
            return isinstance(i, int)

        def has(i):
            return not known(i) or 0 <= i < n_batch

        def ahead(eng, s, value, batch):
            if not known(batch) or batch >= 0:
                eng.wait_ge(s, value)

        def parts(c):
            return (P, IMG, T) if c == 0 else (IMG, 0, IMG)

        @block.sync
        def _(sp):
            for dst, src in ((WT[:, :, :], w_tok.rearrange("(k p) n -> p k n", p=P)),
                             (WQ[:, :, :], w_qkv.rearrange("(k p) n -> p k n", p=P)),
                             (WO[:, :, :], w_out.rearrange("(k p) n -> p k n", p=P)),
                             (WR[:, :, :], router.rearrange("(k p) n -> p k n", p=P)),
                             (WSG[:, :, :], ws_gate_up.rearrange("(k p) n -> p k n", p=P)),
                             (WSD[:, :, :], ws_down.rearrange("(k p) n -> p k n", p=FC)),
                             (POSB[:, :], pos[0, :, :]),
                             (BT[0:1, :], cls[0, :, :]),
                             (BT[1:IMG, :], b_tok.partition_broadcast(IMG - 1)),
                             (GAM[:, :], gamma.partition_broadcast(IMG)),
                             (BET[:, :], beta.partition_broadcast(IMG)),
                             (BO[:, :], b_out.partition_broadcast(P)),
                             (BQ[:, :], b_q), (BK[:, :], b_k), (BV[:, :], b_v)):
                sp.dma_start(dst, src).then_inc(s_wts, 16)
            sp.wait_ge(s_z, 2)
            sp.dma_start(x_rows[tokens:tokens + CAP, :], ZR[:, :]).then_inc(s_zero, 16)
            sp.dma_start(out[tokens:tokens + CAP, :], ZR[:, 0:D]).then_inc(s_zero, 16)
            sp.wait_ge(s_setup, 3)

            def gated():
                sp.sem_inc(s_gate_s, 1)

            def load(b, r):
                ahead(sp, s_fp, FP * (b - 2) + 1, b - 2 if known(b) else b)
                gated()
                sp.dma_start(PT[r % 2][:, :, 1:IMG], patches[bass.ds(b, 1), :, :, :].rearrange("a p k n -> p (a k) n"))\
                    .then_inc(s_patch[r % 2], 16)
                ahead(sp, s_bd, BD * (b - RING) + 3, b - RING if known(b) else b)
                gated()
                sp.dma_start(H[r][:, 0, :], txt[bass.ds(b, 1), :, :].rearrange("a p n -> p (a n)")).then_inc(s_txt[r], 16)

            def diagonal(b):
                sp.wait_ge(s_fa, FA * b + 3)
                gated()
                ahead(sp, s_score, NG * b, b - 1 if known(b) else b)
                gated()
                for h in range(NH):
                    dst, at = (QA, T * h) if h < HALF else (QB, LEAD + T * (h - HALF))
                    p = HD * (h % HALF)
                    sp.dma_start(dst[p:p + HD, at:at + T], QT[p:p + HD, h // HALF, :]).then_inc(s_diag, 16)

            def store(b, r):
                sp.wait_ge(s_bd, BD * b + 16)
                gated()
                sp.dma_start(out[bass.ds(b * T + IMG, TXT), :], OT[r % 2][:, 0, :]).then_inc(s_out[r % 2], 16)
                sp.dma_start(out[bass.ds(b * T, IMG), :], OT[r % 2][0:IMG, 1, :]).then_inc(s_out[r % 2], 16)
                sp.wait_ge(s_bd, BD * b + 20)
                gated()
                sp.dma_start(x_rows[bass.ds(b * T + IMG, TXT), :], X2[r % 2][:, 0, :]).then_inc(s_xrow[r % 2], 16)
                sp.dma_start(x_rows[bass.ds(b * T, IMG), :], X2[r % 2][0:IMG, 1, :]).then_inc(s_xrow[r % 2], 16)

            def iteration(i, r):
                if known(i) and i == -1:
                    load(0, 0)
                if has(i + 2):
                    load(i + 2, (r + 2) % RING)
                if known(i) and i == -1 and n_batch > 0:
                    pass
                if has(i + 1):
                    diagonal(i + 1)
                if has(i - 2):
                    store(i - 2, (r - 2) % RING)

            def load_expert(e, k):
                if k is None or not known(e) or e >= EB:
                    sp.wait_ge(s_ep, 4 * (e - EB + 1))
                gated()
                for w, src, p in ((WG, w_gate, P), (WU, w_up, P), (WD, w_down, FC)):
                    sp.dma_start(w[k][:, :, :], src[bass.ds(e, 1), :, :].rearrange("a (k p) n -> p (a k) n", p=p))\
                        .then_inc(s_ew[k], 16)

            for e in range(EB):
                load_expert(e, e)
            batches(sp, iteration)
            with sp.Fori(1, NE // EB) as n:
                for k in range(EB):
                    load_expert(n * EB + k, k)
            stored(sp)

        @block.gpsimd
        def _(pool):
            done = [0]

            def const(ins):
                done[0] += 1
                ins.then_inc(s_const, 1)

            const(pool.memset(IDENT[:, :], 0.0))
            const(pool.memset(TRI[:, :], 1.0))
            const(pool.memset(ONES[:, :], 1.0))
            const(pool.memset(ONESZ[:, :, :], 0.0))
            const(pool.memset(PAD[:, :, :], 1.0))
            const(pool.memset(PW[:, :], -0.5))
            const(pool.iota(CST[:, :], [[-CAP, NE]], base=FAR, channel_multiplier=0, allow_small_or_imprecise_dtypes=True))
            const(pool.iota(tokf[:, 0:1], [[0, 1]], base=IMG, channel_multiplier=1, allow_small_or_imprecise_dtypes=True))
            const(pool.iota(tokf[:, 1:2], [[0, 1]], base=0, channel_multiplier=1, allow_small_or_imprecise_dtypes=True))
            pool.wait_ge(s_const, done[0])
            const(pool.affine_select(out=IDENT[:, :], in_=IDENT[:, :], compare_op=ALU.not_equal, fill=1.0, base=0,
                                     pattern=[[-1, P]], channel_multiplier=1))
            const(pool.affine_select(out=TRI[:, :], in_=TRI[:, :], compare_op=ALU.is_gt, fill=0.0, base=0,
                                     pattern=[[1, P]], channel_multiplier=-1))
            const(pool.affine_select(out=PAD[:, 1, :], in_=PAD[:, 1, :], compare_op=ALU.is_gt, fill=0.0, base=IMG,
                                     pattern=[[0, NE]], channel_multiplier=-1))
            const(pool.memset(ONESZ[:, 0, 0:HD], 1.0))
            const(pool.memset(ONESZ[:, 1, HD:2 * HD], 1.0))
            pool.memset(ZR[:, :], 0.0).then_inc(s_z, 1)
            ids0 = ids_i[:, :]
            pool.iota(ids0, [[1, CAP]], base=tokens, channel_multiplier=0).then_inc(s_z, 1)
            for t in (QA, QB, PTI):
                const(pool.memset(t[:, :], 0.0))
            for t in VZ + H:
                const(pool.memset(t[:, :, :], 0.0))
            for t in PT:
                const(pool.memset(t[:, :, 0:1], 0.0))
            const(pool.memset(carry[:, :], 0.0))
            const(pool.memset(LT[:, :, :], LOW))
            const(pool.memset(mv[:, :, :], 1.0))
            pool.wait_ge(s_const, done[0])
            pool.wait_ge(s_z, 2)
            pool.dma_start(slot_token.rearrange("(e c) n -> e (c n)", e=NE), ids0).then_inc(s_empty, 16)
            pool.wait_ge(s_empty, 16)
            pool.sem_inc(s_setup, 1)
            pool.wait_ge(s_bo, 3)
            pool.sem_inc(s_setup, 1)
            pool.wait_ge(s_wts, 16 * 15)
            pool.sem_inc(s_setup, 1)

            def gated():
                pool.sem_inc(s_gate_g, 1)

            def front_scale(b):
                pool.wait_ge(s_fd, FD * b + 3)
                gated()
                pool.tensor_scalar(ve[0:IMG, 0:1], mv[0:IMG, 0, 1:2], EPS, None, ALU.add).then_inc(s_fg, 1)
                pool.wait_ge(s_fg, FG * b + 1)
                pool.tensor_tensor(rs[0:IMG, 0:1], ve[0:IMG, 0:1], PW[0:IMG, 0:1], ALU.pow).then_inc(s_fg, 1)

            def front_affine(b, r):
                pool.wait_ge(s_fd, FD * b + 4)
                pool.tensor_tensor(TK[:, :], TK[:, :], GAM[:, :], ALU.mult).then_inc(s_fg, 1)
                ahead(pool, s_bd, BD * (b - RING) + 3, b - RING if known(b) else b)
                pool.wait_ge(s_fg, FG * b + 3)
                pool.tensor_tensor(H[r][0:IMG, 1, :], TK[:, :], BET[:, :], ALU.add).then_inc(s_fg, 1)

            def front_scale2(b):
                pool.wait_ge(s_fd, FD * b + 7)
                gated()
                pool.tensor_scalar(ve[:, :], mv[:, :, 1], EPS, None, ALU.add).then_inc(s_fg, 1)
                pool.wait_ge(s_fg, FG * b + 5)
                pool.tensor_tensor(rs[:, :], ve[:, :], PW[:, :], ALU.pow).then_inc(s_fg, 1)

            def front_bias(b, r):
                pool.wait_ge(s_fd, FD * b + 9)
                pool.tensor_tensor(H[r][:, 0, :], H[r][:, 0, :], BO[:, :], ALU.add).then_inc(s_fg, 1)
                pool.tensor_tensor(H[r][0:IMG, 1, :], H[r][0:IMG, 1, :], BO[0:IMG, :], ALU.add).then_inc(s_fg, 1)

            def front_center(b):
                pool.wait_ge(s_fa, FA * b + 5)
                ahead(pool, s_score, NG * b, b - 1 if known(b) else b)
                gated()
                pool.tensor_scalar(ks[:, :], ks[:, :], -1.0 / T, None, ALU.mult).then_inc(s_fg, 1)
                pool.wait_ge(s_fg, FG * b + 9)
                gated()
                for k in range(KC):
                    last = pool.tensor_scalar(KZ[:, k, :], KT[:, k, :], ks[:, k:k + 1], 1.0, ALU.add, ALU.mult)
                last.then_inc(s_fg, 1)

            def back_scale(b):
                pool.wait_ge(s_bd, BD * b + 7)
                gated()
                pool.tensor_scalar(bve[:, :], bmv[:, :, 1], EPS, None, ALU.add).then_inc(s_bg, 1)
                pool.wait_ge(s_bg, BG * b + 1)
                pool.tensor_tensor(brs[:, :], bve[:, :], PW[:, :], ALU.pow).then_inc(s_bg, 1)

            def back_slots(b, r):
                ahead(pool, s_slot[r % 2], of_ring(b - 2, r % 2, 2, SL), b - 2 if known(b) else b)
                pool.wait_ge(s_bg, BG * b + 2)
                gated()
                pool.tensor_copy(TOKI[r % 2][:, :], tokf[:, :]).then_inc(s_bg, 1)
                pool.wait_ge(s_bg, BG * b + 3)
                gated()
                pool.tensor_scalar(tokf[:, :], tokf[:, :], float(T), None, ALU.add).then_inc(s_bg, 1)
                pool.wait_ge(s_bd, BD * b + 28)
                gated()
                for c, n in ((1, IMG), (0, P)):
                    for k in range(8):
                        pool.indirect_dma_start(slot_token, bass.IndirectOffsetOnAxis(SLOT[r % 2][0:n, c, k:k + 1], 0),
                                                TOKI[r % 2][0:n, c:c + 1], None, bounds_check=SLOTS - 1,
                                                oob_is_err=False).then_inc(s_slot[r % 2], 16)

            def iteration(i, r):
                f, b = has(i + 1), has(i - 2)
                if f:
                    front_scale(i + 1)
                    front_affine(i + 1, (r + 1) % RING)
                if b:
                    back_scale(i - 2)
                if f:
                    front_scale2(i + 1)
                    front_bias(i + 1, (r + 1) % RING)
                    front_center(i + 1)
                if b:
                    back_slots(i - 2, (r - 2) % RING)

            batches(pool, iteration)
            for n in range(2):
                pool.wait_ge(s_slot[n], SL * len(range(n, n_batch, 2)))
            pool.dma_start(ids_i[:, :], slot_token.rearrange("(e c) n -> e (c n)", e=NE)).then_inc(s_ids, 16)

            def gather(e, k):
                pool.wait_ge(s_ix, e + 1)
                gated()
                pool.indirect_dma_start(XG[k][:, :], None, x_rows, bass.IndirectOffsetOnAxis(IX[k][:, :], 0))\
                    .then_inc(s_xg[k], 16)

            def add(e, k):
                pool.wait_ge(s_ed, 3 * e + 3)
                ahead(pool, s_add, 16 * e, e)
                gated()
                pool.indirect_dma_start(out, bass.IndirectOffsetOnAxis(IX[k][:, :], 0), Y[k][:, :], None,
                                        compute_op=ALU.add).then_inc(s_add, 16)

            stored(pool)
            def expert(e, k):
                if not known(e) or e + 2 < NE:
                    gather(e + 2, (k + 2) % EB)
                add(e, k)

            gather(0, 0)
            gather(1, 1)
            experts(pool, expert)
            pool.wait_ge(s_add, 16 * NE)

        @block.scalar
        def _(act):
            act.wait_ge(s_setup, 3)

            def front_xt(b):
                act.wait_ge(s_fp, FP * b + 2)
                act.activation(XT[:, :, :], chunks(bF, KC, T), ACT.Copy).then_inc(s_fa, 1)

            def front_q(b):
                act.wait_ge(s_fp, FP * b + 3)
                ahead(act, s_diag, DG * b, b - 1 if known(b) else b)
                for k in range(KC):
                    act.activation(QT[:, k, :], chunks(bF, KC, T)[:, k, :], ACT.Identity, bias=BQ[:, k:k + 1]).then_inc(s_fa, 1)

            def front_k(b):
                act.wait_ge(s_fp, FP * b + 4)
                ahead(act, s_fg, FG * b, b - 1 if known(b) else b)
                for k in range(KC):
                    act.activation(KT[:, k, :], chunks(bF, KC, T)[:, k, :], ACT.Identity, bias=BK[:, k:k + 1],
                                   accum_out=ks[:, k:k + 1]).then_inc(s_fa, 1)

            def front_v(b, r):
                act.wait_ge(s_fp, FP * b + 5)
                ahead(act, s_bp, BP * (b - RING) + 1, b - RING if known(b) else b)
                for c in range(2):
                    n = parts(c)[0]
                    v = chunks(bF, 2, D)[0:n, c, :].rearrange("p (g a d) -> p g a d", g=HALF, a=2)
                    z = VZ[r][0:n, c, :].rearrange("p (g x) -> p g x", g=HALF)
                    for a in range(2):
                        last = act.activation(z[:, :, 3 * HD * a:3 * HD * a + HD], v[:, :, a, :], ACT.Copy)
                last.then_inc(s_fa, 1)

            def exps(i, r):
                for g in range(NG):
                    act.wait_ge(s_take, NT * i + GROUP * (g + 1))
                    act.activation(nb[:, GROUP * g:GROUP * (g + 1)], mx[:, GROUP * g:GROUP * (g + 1)], ACT.Copy,
                                   scale=-SCALE).then_inc(s_exp, 1)
                    if g == 0:
                        ahead(act, s_tr, TR_N * (i - 1), i - 2 if known(i) else i)
                    act.wait_ge(s_exp, EX_N * i + (GROUP + 1) * g + 1)
                    for t in range(GROUP * g, GROUP * (g + 1)):
                        act.activation(E[r % 2][:, t, :], chunks(bS[g % 3], GROUP, T)[:, t % GROUP, :], ACT.Exp,
                                       bias=nb[:, t:t + 1], scale=SCALE).then_inc(s_exp, 1)

            def transposed(i):
                for n in range(TRC_N // 2):
                    w = min(4, NT - 4 * n) * P
                    act.wait_ge(s_tr, TR_N * i + min(4 * n + 4, NT))
                    if n == 0:
                        ahead(act, s_bp, BP * (i - 1) + 2, i - 1 if known(i) else i)
                    act.activation(PTT[:, 4 * P * n:4 * P * n + w], bT[:, 0:w], ACT.Copy).then_inc(s_trc, 1)
                    act.activation(PTI[0:IMG, 4 * P * n:4 * P * n + w], bI[0:IMG, 0:w], ACT.Copy).then_inc(s_trc, 1)

            def back_xt(b):
                act.wait_ge(s_bp, BP * b + 4)
                act.activation(X2T[:, :, :], chunks(bY, KC, T), ACT.Copy).then_inc(s_ba, 1)

            def back_tanh(b):
                act.wait_ge(s_bp, BP * b + 5)
                act.activation(TH[:, :, :], chunks(bX, NF, T)[0:FC], ACT.Tanh, scale=0.5).then_inc(s_ba, 1)

            def back_weights(b):
                act.wait_ge(s_bd, BD * b + 15)
                act.activation(nl[:, :], L8[:, :, 0], ACT.Copy, scale=-1.0).then_inc(s_ba, 1)
                act.wait_ge(s_ba, BA * b + 3)
                for c in range(2):
                    act.activation(EX[:, c, :], chunks(bY, 2, NE)[:, c, :], ACT.Exp, bias=nl[:, c:c + 1]).then_inc(s_ba, 1)
                for c in range(2):
                    act.activation(e8[:, c, :], L8[:, c, :], ACT.Exp, bias=nl[:, c:c + 1],
                                   accum_out=s8[:, c:c + 1]).then_inc(s_ba, 1)

            def iteration(i, r):
                f, b = has(i + 1), has(i - 2)
                if has(i):
                    exps(i, r)
                if f:
                    front_xt(i + 1)
                if b:
                    back_xt(i - 2)
                if f:
                    front_q(i + 1)
                if b:
                    back_tanh(i - 2)
                if f:
                    front_k(i + 1)
                    front_v(i + 1, (r + 1) % RING)
                if b:
                    back_weights(i - 2)
                if has(i - 1):
                    transposed(i - 1)

            batches(act, iteration)

            def expert(e, k):
                act.wait_ge(s_ep, 4 * e + 1)
                act.activation(XE[:, :, :], chunks(bT, KC, P), ACT.Copy).then_inc(s_ea, 1)
                act.wait_ge(s_ep, 4 * e + 2)
                act.activation(TE[:, :, :], chunks(bX, NF, P)[0:FC], ACT.Tanh, scale=0.5).then_inc(s_ea, 1)

            experts(act, expert)

        @block.vector
        def _(dve):
            dve.wait_ge(s_wts, 16 * 15)
            dve.tensor_tensor(POSB[:, :], POSB[:, :], BT[:, :], ALU.add).then_inc(s_bo, 1)
            dve.tensor_copy(BVR[:, :, :], BV[:, :].rearrange("p (k a) -> p k a", a=1).to_broadcast([P, KC, P])).then_inc(s_bo, 1)
            dve.wait_ge(s_bv, 1)
            dve.tensor_tensor(BO[:, :], BO[:, :], bX[:, 0:D], ALU.add).then_inc(s_bo, 1)
            dve.wait_ge(s_setup, 3)

            def gated():
                dve.sem_inc(s_gate_d, 1)

            def step(s, n, b):
                def upto(k):
                    dve.wait_ge(s, n * b + k)
                return upto

            def front_embed(b):
                seen = step(s_fd, FD, b)
                dve.wait_ge(s_fp, FP * b + 1)
                ahead(dve, s_fg, FG * b, b - 1 if known(b) else b)
                dve.tensor_tensor(TK[:, :], bF[0:IMG, 0:D], POSB[:, :], ALU.add).then_inc(s_fd, 1)
                seen(1)
                dve.bn_stats(st[0:IMG, 0, :], TK[:, :]).then_inc(s_fd, 1)
                seen(2)
                gated()
                dve.bn_aggr(mv[0:IMG, 0, :], st[0:IMG, 0, :]).then_inc(s_fd, 1)

            def front_embed2(b):
                dve.wait_ge(s_fg, FG * b + 2)
                dve.tensor_scalar(TK[:, :], TK[:, :], mv[0:IMG, 0, 0:1], rs[0:IMG, 0:1], ALU.subtract, ALU.mult).then_inc(s_fd, 1)

            def front_norm(b, r):
                dve.wait_ge(s_txt[r], of_ring(b, r, RING, 16))
                dve.wait_ge(s_fd, FD * b + 4)
                dve.bn_stats(st[:, 0, :], H[r][:, 0, :]).then_inc(s_fd, 1)
                dve.wait_ge(s_fg, FG * b + 4)
                dve.bn_stats(st[0:IMG, 1, :], H[r][0:IMG, 1, :]).then_inc(s_fd, 1)
                dve.wait_ge(s_fd, FD * b + 6)
                gated()
                dve.bn_aggr(mv[:, 0, :], st[:, 0, :])
                dve.bn_aggr(mv[0:IMG, 1, :], st[0:IMG, 1, :]).then_inc(s_fd, 1)

            def front_norm2(b, r):
                dve.wait_ge(s_fg, FG * b + 6)
                ahead(dve, s_fp, FP * (b - 1) + 2, b - 1 if known(b) else b)
                dve.tensor_scalar(XN[:, 0, :], H[r][:, 0, :], mv[:, 0, 0:1], rs[:, 0:1], ALU.subtract, ALU.mult).then_inc(s_fd, 1)
                dve.tensor_scalar(XN[0:IMG, 1, :], H[r][0:IMG, 1, :], mv[0:IMG, 1, 0:1], rs[0:IMG, 1:2],
                                  ALU.subtract, ALU.mult).then_inc(s_fd, 1)

            def take(i, r):
                for t in range(NT):
                    g = t // GROUP
                    if t == 0:
                        ahead(dve, s_prob, NT * (i - 1), i - 2 if known(i) else i)
                        ahead(dve, s_exp, EX_N * i, i - 1 if known(i) else i)
                    if t % GROUP == 0:
                        dve.wait_ge(s_score, NG * i + g + 1)
                    dve.tensor_scalar(S[r % 2][:, t, :], chunks(bS[g % 3], GROUP, T)[:, t % GROUP, :], 1.0, None,
                                      ALU.mult, ALU.max, accum_out=mx[:, t:t + 1]).then_inc(s_take, 1)

            def select(i, r, between):
                W = S[r % 2]
                at = [TOP_N * i]
                n = 0
                dve.wait_ge(s_take, NT * (i + 1))
                gated()
                for rnd in range(ROUNDS + 1):
                    for t in range(NT):
                        if rnd and t % 7 == 0:
                            dve.wait_ge(s_top, at[0] + NT * (2 * rnd - 1) + t + 7)
                            gated()
                        dve.max(M8[:, t, :], W[:, t, :]).then_inc(s_top, 1)
                        n += 1
                        if n % 16 == 0 and between:
                            between.pop(0)()
                    if rnd == ROUNDS:
                        break
                    for t in range(NT):
                        if t % 7 == 0:
                            dve.wait_ge(s_top, at[0] + NT * 2 * rnd + t + 7)
                            gated()
                        dve.match_replace(W[:, t, :], M8[:, t, :], W[:, t, :], LOW).then_inc(s_top, 1)
                        n += 1
                        if n % 16 == 0 and between:
                            between.pop(0)()
                while between:
                    between.pop(0)()
                n = NT * (2 * ROUNDS + 1)
                dve.wait_ge(s_top, at[0] + n)
                dve.tensor_copy(LT[:, :, 0], M8[:, :, 0]).then_inc(s_top, 1)
                dve.wait_ge(s_top, at[0] + n + 1)
                gated()
                for t in range(NT):
                    dve.match_replace(W[:, t, :], LT[:, t, :], W[:, t, :], LOW).then_inc(s_top, 1)

            def mask(i, r):
                for t in range(NT):
                    if t == 0:
                        dve.wait_ge(s_exp, EX_N * (i + 1))
                    dve.wait_ge(s_top, TOP_N * (i + 1) - NT + t + 1)
                    dve.scalar_tensor_tensor(E[r % 2][:, t, :], S[r % 2][:, t, :], GONE, E[r % 2][:, t, :],
                                             ALU.is_lt, ALU.mult).then_inc(s_prob, 1)

            def back_ctx(b, r):
                seen = step(s_bd, BD, b)
                dve.wait_ge(s_bp, BP * b + 2)
                dve.reciprocal(RD[:, :, :], chunks(bY, KC, T)).then_inc(s_bd, 1)
                seen(1)
                dve.tensor_tensor(CT[:, :, :], chunks(bX, KC, T), RD[:, :, :], ALU.mult).then_inc(s_bd, 1)

            def back_res(b, r):
                seen = step(s_bd, BD, b)
                dve.wait_ge(s_bp, BP * b + 3)
                dve.tensor_tensor(HM[:, :, :], chunks(bX, 2, D), H[r][:, :, :], ALU.add).then_inc(s_bd, 1)
                seen(3)
                dve.bn_stats(bst[:, 0, :], HM[:, 0, :]).then_inc(s_bd, 1)
                dve.bn_stats(bst[:, 1, :], HM[:, 1, :]).then_inc(s_bd, 1)
                seen(5)
                gated()
                dve.bn_aggr(bmv[:, 0, :], bst[:, 0, :]).then_inc(s_bd, 1)
                dve.bn_aggr(bmv[:, 1, :], bst[:, 1, :]).then_inc(s_bd, 1)

            def back_norm(b, r):
                dve.wait_ge(s_bg, BG * b + 2)
                ahead(dve, s_xrow[r % 2], of_ring(b - 2, r % 2, 2, 32), b - 2 if known(b) else b)
                for c in range(2):
                    dve.tensor_scalar(X2[r % 2][:, c, 0:D], HM[:, c, :], bmv[:, c, 0:1], brs[:, c:c + 1],
                                      ALU.subtract, ALU.mult).then_inc(s_bd, 1)

            def back_glu(b):
                seen = step(s_bd, BD, b)
                dve.wait_ge(s_ba, BA * b + 2)
                g, u = chunks(bX, NF, T)[0:FC], chunks(bY, NF, T)[0:FC]
                dve.scalar_tensor_tensor(TH[:, :, :], TH[:, :, :], 1.0, g, ALU.add, ALU.mult).then_inc(s_bd, 1)
                seen(10)
                dve.wait_ge(s_bp, BP * b + 6)
                dve.scalar_tensor_tensor(HT[:, :, :], TH[:, :, :], 0.5, u, ALU.mult, ALU.mult).then_inc(s_bd, 1)

            def back_top(b):
                seen = step(s_bd, BD, b)
                dve.wait_ge(s_bp, BP * b + 8)
                gated()
                for c in range(2):
                    dve.max(L8[:, c, :], chunks(bY, 2, NE)[:, c, :]).then_inc(s_bd, 1)
                seen(13)
                gated()
                for c in range(2):
                    dve.match_replace(MR[:, c, :], L8[:, c, :], chunks(bY, 2, NE)[:, c, :], LOW).then_inc(s_bd, 1)

            def back_out(b, r):
                ahead(dve, s_out[r % 2], of_ring(b - 2, r % 2, 2, 32), b - 2 if known(b) else b)
                dve.wait_ge(s_bp, BP * b + 7)
                dve.tensor_tensor(OT[r % 2][:, :, :], chunks(bX, 2, D), HM[:, :, :], ALU.add).then_inc(s_bd, 1)
                dve.wait_ge(s_bd, BD * b + 15)
                dve.scalar_tensor_tensor(MK[:, :, :], MR[:, :, :], GONE, PAD[:, :, :], ALU.is_lt, ALU.mult).then_inc(s_bd, 1)

            def back_weights(b, r):
                seen = step(s_bd, BD, b)
                dve.wait_ge(s_ba, BA * b + 7)
                dve.reciprocal(r8[:, :], s8[:, :]).then_inc(s_bd, 1)
                seen(18)
                for c in range(2):
                    dve.tensor_scalar(X2[r % 2][:, c, D:XW], EX[:, c, :], r8[:, c:c + 1], None, ALU.mult).then_inc(s_bd, 1)

            def back_slots(b, r):
                seen = step(s_bd, BD, b)
                dve.wait_ge(s_bp, BP * b + 9)
                cum = bY[:, 2 * NE:5 * NE].rearrange("p (c n) -> p c n", c=3)
                cb = carry[:, :].rearrange("p (a n) -> p a n", a=1).to_broadcast([P, 2, NE])
                dve.tensor_tensor(PO[:, :, :], cum[:, 0:2, :], cb, ALU.add).then_inc(s_bd, 1)
                seen(21)
                dve.tensor_tensor(carry[:, :], cum[:, 2, :], carry[:, :], ALU.add).then_inc(s_bd, 1)
                dve.scalar_tensor_tensor(KEEP[:, :, :], PO[:, :, :], float(CAP), MK[:, :, :], ALU.is_lt, ALU.mult).then_inc(s_bd, 1)
                for c in range(2):
                    last = dve.scalar_tensor_tensor(MR[:, c, :], PO[:, c, :], -1.0, CST[:, :], ALU.mult, ALU.add)
                last.then_inc(s_bd, 1)
                seen(24)
                dve.tensor_tensor(MR[:, :, :], MR[:, :, :], KEEP[:, :, :], ALU.mult).then_inc(s_bd, 1)
                seen(25)
                gated()
                for c in range(2):
                    dve.max(N8[:, c, :], MR[:, c, :]).then_inc(s_bd, 1)
                ahead(dve, s_slot[r % 2], of_ring(b - 2, r % 2, 2, SL), b - 2 if known(b) else b)
                seen(27)
                dve.tensor_scalar(SLOT[r % 2][:, :, :], N8[:, :, :], -1.0, float(FAR), ALU.mult, ALU.add).then_inc(s_bd, 1)

            def iteration(i, r):
                f, b = has(i + 1), has(i - 2)
                rf, rb = (r + 1) % RING, (r - 2) % RING
                steps = []
                if b:
                    steps += [lambda: back_ctx(i - 2, rb)]
                if f:
                    steps += [lambda: front_embed(i + 1), lambda: front_embed2(i + 1)]
                if b:
                    steps += [lambda: back_res(i - 2, rb), lambda: back_norm(i - 2, rb)]
                if f:
                    steps += [lambda: front_norm(i + 1, rf), lambda: front_norm2(i + 1, rf)]
                if b:
                    steps += [lambda: back_glu(i - 2), lambda: back_top(i - 2), lambda: back_out(i - 2, rb),
                              lambda: back_weights(i - 2, rb), lambda: back_slots(i - 2, rb)]
                if has(i):
                    take(i, r)
                if has(i - 1):
                    select(i - 1, (r - 1) % RING, steps)
                    mask(i - 1, (r - 1) % RING)
                for s in steps:
                    s()

            batches(dve, iteration)

            dve.wait_ge(s_ids, 16)
            dve.tensor_copy(ids_f[:, :], ids_i[:, :]).then_inc(s_idt, 1)
            dve.wait_ge(s_idp, 1)
            dve.tensor_copy(ids_t[:, :], bI[:, 0:NE]).then_inc(s_idt, 1)
            dve.wait_ge(s_idt, 2)

            def index(e, k):
                ahead(dve, s_add, 16 * (e - EB + 1), e - EB if known(e) else e)
                dve.tensor_copy(IX[k][:, :], ids_t[:, bass.ds(e, 1)]).then_inc(s_ix, 1)

            def expert(e, k):
                g, u = chunks(bX, NF, P)[0:FC], chunks(bY, NF, P)[0:FC]
                dve.wait_ge(s_ea, 2 * e + 2)
                dve.scalar_tensor_tensor(TG[:, :, :], TE[:, :, :], 1.0, g, ALU.add, ALU.mult).then_inc(s_ed, 1)
                dve.wait_ge(s_ep, 4 * e + 3)
                dve.wait_ge(s_ed, 3 * e + 1)
                dve.scalar_tensor_tensor(HE[:, :, :], TG[:, :, :], 0.5, u, ALU.mult, ALU.mult).then_inc(s_ed, 1)
                dve.wait_ge(s_ep, 4 * e + 4)
                dve.tensor_scalar(Y[k][:, :], bF[:, 0:D], XG[k][:, bass.ds(e + D, 1)], None, ALU.mult).then_inc(s_ed, 1)

            def both(e, k):
                expert(e, k)
                if not known(e) or e + 2 < NE:
                    index(e + 2, (k + 2) % EB)

            index(0, 0)
            index(1, 1)
            experts(dve, both)

        @block.tensor
        def _(pe):
            pe.wait_ge(s_bo, 2)
            for k in range(KC):
                last = pe.matmul(bX[:, 0:D], BVR[:, k, :], WO[:, k, :], start=(k == 0), stop=(k == KC - 1))
            last.then_inc(s_bv, 1)
            pe.wait_ge(s_setup, 3)

            def front_embed(b, r):
                pe.wait_ge(s_patch[r % 2], of_ring(b, r % 2, 2, 16))
                ahead(pe, s_fa, FA * b, b - 1 if known(b) else b)
                for k in range(PK):
                    last = pe.matmul(bF[0:IMG, 0:D], PT[r % 2][:, k, :], WT[:, k, :], start=(k == 0), stop=(k == PK - 1))
                last.then_inc(s_fp, 1)

            def front_xt(b):
                pe.wait_ge(s_fd, FD * b + 9)
                for c in range(2):
                    n, lo, hi = parts(c)
                    for k in range(KC):
                        last = pe.transpose(chunks(bF, KC, T)[:, k, lo:hi], XN[0:n, c, P * k:P * k + P], IDENT[0:n, 0:n])
                last.then_inc(s_fp, 1)

            def front_qk(b, which):
                pe.wait_ge(s_fa, FA * b + (1 if which == 0 else 3))
                for m in range(KC):
                    for k in range(KC):
                        at = D * which + P * m
                        last = pe.matmul(chunks(bF, KC, T)[:, m, :], WQ[:, k, at:at + P], XT[:, k, :],
                                         start=(k == 0), stop=(k == KC - 1))
                last.then_inc(s_fp, 1)

            def front_v(b):
                pe.wait_ge(s_fa, FA * b + 5)
                for c in range(2):
                    n, lo, hi = parts(c)
                    for k in range(KC):
                        last = pe.matmul(chunks(bF, 2, D)[0:n, c, :], XT[:, k, lo:hi], WQ[:, k, 2 * D:3 * D],
                                         start=(k == 0), stop=(k == KC - 1))
                last.then_inc(s_fp, 1)

            def scores(i):
                pe.wait_ge(s_diag, DG * (i + 1))
                pe.wait_ge(s_fg, FG * (i + 1))
                for g in range(NG):
                    if g >= 3:
                        pe.wait_ge(s_take, NT * i + GROUP * (g - 2))
                        pe.wait_ge(s_exp, EX_N * i + (GROUP + 1) * (g - 2))
                    elif g == 0:
                        ahead(pe, s_take, NT * i, i - 1 if known(i) else i)
                        ahead(pe, s_exp, EX_N * i, i - 1 if known(i) else i)
                    for t in range(GROUP * g, GROUP * (g + 1)):
                        o = chunks(bS[g % 3], GROUP, T)[:, t % GROUP, :]
                        if t <= MIXED:
                            last = pe.matmul(o, QA[:, P * t:P * t + P], KZ[:, 0, :], start=True, stop=(t < MIXED))
                        if t >= MIXED:
                            at = P * (t - MIXED)
                            last = pe.matmul(o, QB[:, at:at + P], KZ[:, 1, :], start=(t > MIXED), stop=True)
                    last.then_inc(s_score, 1)

            def transposes(i, r):
                for t in range(NT):
                    n = t // 4
                    pe.wait_ge(s_prob, NT * i + t + 1)
                    if t % 4 == 0:
                        ahead(pe, s_trc, TRC_N * i + 2 * n, i if n else (i - 1 if known(i) else i))
                    at = P * (t % 4)
                    pe.transpose(bT[:, at:at + P], E[r % 2][:, t, IMG:T], IDENT[:, :])
                    pe.transpose(bI[0:IMG, at:at + P], E[r % 2][:, t, 0:IMG], IDENT[:, :]).then_inc(s_tr, 1)

            def context(i, r):
                pe.wait_ge(s_trc, TRC_N * (i + 1))
                ahead(pe, s_bd, BD * i, i - 1 if known(i) else i)
                for out_b, what in ((bX, "values"), (bY, "sums")):
                    for hf in range(KC):
                        o = chunks(out_b, KC, T)[:, hf, :]
                        for n, (a, c) in enumerate(((0, 0), (0, 1), (1, 0), (1, 1))):
                            for g in range(4):
                                h = HALF * hf + 2 * g + a
                                p = (PTT, PTI)[c][:, T * h:T * h + T]
                                w = VZ[r][:, c, 2 * HD * h:2 * HD * (h + 1)] if what == "values" else ONESZ[:, a, :]
                                last = pe.matmul(o[2 * HD * g:2 * HD * (g + 1)], w, p, start=(n == 0), stop=(n == 3),
                                                 skip_group_check=True)
                    last.then_inc(s_bp, 1)

            def back_proj(b):
                pe.wait_ge(s_bd, BD * b + 2)
                for c in range(2):
                    lo = IMG if c == 0 else 0
                    for k in range(KC):
                        last = pe.matmul(chunks(bX, 2, D)[:, c, :], CT[:, k, lo:lo + P], WO[:, k, :],
                                         start=(k == 0), stop=(k == KC - 1))
                last.then_inc(s_bp, 1)

            def back_xt(b, r):
                pe.wait_ge(s_bd, BD * b + 9)
                for c in range(2):
                    n, lo, hi = parts(c)
                    for k in range(KC):
                        last = pe.transpose(chunks(bY, KC, T)[:, k, lo:hi], X2[r % 2][0:n, c, P * k:P * k + P], IDENT[0:n, 0:n])
                last.then_inc(s_bp, 1)

            def back_glu(b):
                pe.wait_ge(s_ba, BA * b + 1)
                for n, bank in enumerate((bX, bY)):
                    for f in range(NF):
                        for k in range(KC):
                            at = FF * n + FC * f
                            last = pe.matmul(chunks(bank, NF, T)[0:FC, f, :], WSG[:, k, at:at + FC], X2T[:, k, :],
                                             start=(k == 0), stop=(k == KC - 1))
                    last.then_inc(s_bp, 1)

            def back_down(b):
                pe.wait_ge(s_bd, BD * b + 11)
                for c in range(2):
                    lo = IMG if c == 0 else 0
                    for f in range(NF):
                        last = pe.matmul(chunks(bX, 2, D)[:, c, :], HT[:, f, lo:lo + P], WSD[:, f, :],
                                         start=(f == 0), stop=(f == NF - 1))
                last.then_inc(s_bp, 1)
                for c in range(2):
                    lo = IMG if c == 0 else 0
                    for k in range(KC):
                        last = pe.matmul(chunks(bY, 2, NE)[:, c, :], X2T[:, k, lo:lo + P], WR[:, k, :],
                                         start=(k == 0), stop=(k == KC - 1))
                last.then_inc(s_bp, 1)

            def back_count(b):
                pe.wait_ge(s_bd, BD * b + 17)
                pe.wait_ge(s_ba, BA * b + 5)
                cum = bY[:, 2 * NE:5 * NE].rearrange("p (c n) -> p c n", c=3)
                pe.matmul(cum[:, 0, :], TRI[:, :], MK[:, 0, :], start=True, stop=False)
                pe.matmul(cum[:, 0, :], ONES[:, :], MK[:, 1, :], start=False, stop=True)
                pe.matmul(cum[:, 1, :], TRI[:, :], MK[:, 1, :], start=True, stop=True)
                pe.matmul(cum[:, 2, :], ONES[:, :], MK[:, 0, :], start=True, stop=False)
                pe.matmul(cum[:, 2, :], ONES[:, :], MK[:, 1, :], start=False, stop=True).then_inc(s_bp, 1)

            def iteration(i, r):
                f, b = has(i + 1), has(i - 2)
                rf, rb = (r + 1) % RING, (r - 2) % RING
                if has(i):
                    scores(i)
                if f:
                    front_embed(i + 1, rf)
                if b:
                    back_proj(i - 2)
                if f:
                    front_xt(i + 1)
                if b:
                    back_xt(i - 2, rb)
                if f:
                    front_qk(i + 1, 0)
                if b:
                    back_glu(i - 2)
                if f:
                    front_qk(i + 1, 1)
                if b:
                    back_down(i - 2)
                if f:
                    front_v(i + 1)
                if b:
                    back_count(i - 2)
                if has(i - 1):
                    transposes(i - 1, (r - 1) % RING)
                    context(i - 1, (r - 1) % RING)

            batches(pe, iteration)

            pe.wait_ge(s_idt, 1)
            pe.transpose(bI[:, 0:NE], ids_f[:, :], IDENT[0:NE, 0:NE]).then_inc(s_idp, 1)

            def expert(e, k):
                pe.wait_ge(s_xg[k], of_ring(e, k, EB, 16))
                for c in range(KC):
                    last = pe.transpose(chunks(bT, KC, P)[:, c, :], XG[k][:, P * c:P * c + P], IDENT[:, :])
                last.then_inc(s_ep, 1)
                pe.wait_ge(s_ea, 2 * e + 1)
                pe.wait_ge(s_ew[k], of_ring(e, k, EB, 48))
                for n, (bank, w) in enumerate(((bX, WG[k]), (bY, WU[k]))):
                    for f in range(NF):
                        for c in range(KC):
                            last = pe.matmul(chunks(bank, NF, P)[0:FC, f, :], w[:, c, FC * f:FC * f + FC], XE[:, c, :],
                                             start=(c == 0), stop=(c == KC - 1))
                    last.then_inc(s_ep, 1)
                pe.wait_ge(s_ed, 3 * e + 2)
                for f in range(NF):
                    last = pe.matmul(bF[:, 0:D], HE[:, f, :], WD[k][:, f, :], start=(f == 0), stop=(f == NF - 1))
                last.then_inc(s_ep, 1)

            experts(pe, expert)


def kernel(x, txt, L0_tok_W, L0_tok_b, L0_tok_cls_token, L0_tok_pos_embedding, L0_tok_gamma, L0_tok_beta,
           L0_attn_W_qkv, L0_attn_b_qkv, L0_attn_W_out, L0_attn_b_out, L0_ffn_router_w, L0_ffn_w_gate, L0_ffn_w_up,
           L0_ffn_w_down, L0_ffn_ws_gate_up, L0_ffn_ws_down):
    import numpy as np
    import concourse.bacc as bacc
    from concourse.bass_utils import run_bass_kernel_spmd

    n_batch = x.shape[0]
    patches = np.asarray(x).reshape(n_batch, 3, 6, 16, 6, 16).transpose(0, 1, 3, 5, 2, 4).reshape(n_batch, PK, P, IMG - 1)
    bq, bk, bv = (np.asarray(L0_attn_b_qkv)[D * n:D * (n + 1)].reshape(KC, P).T for n in range(3))
    named = dict(patches=patches.transpose(0, 2, 1, 3), txt=txt, w_tok=L0_tok_W, b_tok=L0_tok_b, cls=L0_tok_cls_token,
                 pos=L0_tok_pos_embedding, gamma=L0_tok_gamma, beta=L0_tok_beta, w_qkv=np.asarray(L0_attn_W_qkv).T,
                 b_q=bq, b_k=bk, b_v=bv, w_out=np.asarray(L0_attn_W_out).T, b_out=L0_attn_b_out,
                 router=np.asarray(L0_ffn_router_w).T, w_gate=L0_ffn_w_gate, w_up=L0_ffn_w_up, w_down=L0_ffn_w_down,
                 ws_gate_up=L0_ffn_ws_gate_up, ws_down=L0_ffn_ws_down)
    nc = bacc.Bacc("TRN2", target_bir_lowering=False, num_devices=1)
    arrays = {f"in_{k}": np.ascontiguousarray(v) for k, v in named.items()}
    args = {k: nc.dram_tensor(f"in_{k}", arrays[f"in_{k}"].shape, fp32, kind="ExternalInput").ap() for k in named}
    out = nc.dram_tensor("out", (n_batch * T + CAP, D), fp32, kind="ExternalOutput").ap()
    early_fusion_kernel(nc, *args.values(), out, n_batch)
    r = run_bass_kernel_spmd(nc, [arrays], core_ids=[0])
    return r.results[0]["out"][0:n_batch * T].reshape(n_batch, T, D)
```

```python
import concourse.bass as bass
from concourse import mybir
from contextlib import ExitStack

fp32 = mybir.dt.float32
i32 = mybir.dt.int32
u32 = mybir.dt.uint32
ALU = mybir.AluOpType
ACT = mybir.ActivationFunctionType
AX = mybir.AxisListType

P = 128
D = 256
KC = D // P
IMG = 37
TXT = 128
T = IMG + TXT
PK = 768 // P
NH = 16
HD = D // NH
HALF = NH // 2
ROWS = NH * T
NT = -(-ROWS // P)
HROWS = HALF * T
MIXED = HROWS // P
LEAD = HROWS - MIXED * P
QW = (MIXED + 1) * P
GROUP = 3
NG = NT // GROUP
AHEAD = 4 * GROUP
TOPK = int(T * 0.3)
ROUNDS = TOPK // 8
WIN = 16
AIM = TOPK - WIN / 2 + 0.5
GUESS = 0.676
SLOPE = 1.0 / 65.0
NEAR = 6.9 * 6.9
NE = 64
FF = 192
FC = 96
NF = FF // FC
CAP = 128
SLOTS = NE * CAP
FAR = 2 * SLOTS
XW = D + NE
RING = 4
FIRST = 5
EB = 4
EPS = 1e-5
SCALE = float(D) ** -0.5
LOW = -3.0e38
GONE = -1.0e38
assert TOPK == 8 * ROUNDS + 1 and NT % GROUP == 0


def early_fusion_kernel(nc, patches, txt, w_tok, b_tok, cls, pos, gamma, beta, w_qkv, b_q, b_k, b_v, w_out, b_out,
                        router, w_gate, w_up, w_down, ws_gate_up, ws_down, out, n_batch):
    tokens = n_batch * T
    ctx = ExitStack()
    with ctx:
        def sb(name, shape, dt=fp32):
            return ctx.enter_context(nc.sbuf_tensor(name, shape, dt))

        def sem(name):
            return ctx.enter_context(nc.semaphore(name))

        x_rows = nc.dram_tensor("x_rows", (tokens + CAP, XW), fp32).ap()
        slot_token = nc.dram_tensor("slot_token", (SLOTS, 1), i32).ap()

        WT = sb("WT", [P, PK, D])
        WQ = sb("WQ", [P, KC, 3 * D])
        WO = sb("WO", [P, KC, D])
        WR = sb("WR", [P, KC, NE])
        WSG = sb("WSG", [P, KC, 2 * FF])
        WSD = sb("WSD", [FC, NF, D])
        POSB = sb("POSB", [IMG, D])
        BT = sb("BT", [IMG, D])
        GAM = sb("GAM", [IMG, D])
        BET = sb("BET", [IMG, D])
        BQ = sb("BQ", [P, KC])
        BK = sb("BK", [P, KC])
        BV = sb("BV", [P, KC])
        BVR = sb("BVR", [P, KC, P])
        BO = sb("BO", [P, D])
        IDENT = sb("IDENT", [P, P])
        TRI = sb("TRI", [P, P])
        ONES = sb("ONES", [P, P])
        ONESZ = sb("ONESZ", [P, 2, 2 * HD])
        PAD = sb("PAD", [P, 2, NE])
        CST = sb("CST", [P, NE])
        PW = sb("PW", [P, 2])
        ZR = sb("ZR", [P, XW])
        PT = [sb(f"PT{n}", [P, PK, IMG]) for n in range(2)]
        H = [sb(f"H{n}", [P, 2, D]) for n in range(RING)]
        TK = sb("TK", [IMG, D])
        st = sb("st", [P, 2, 6])
        mv = sb("mv", [P, 2, 2])
        ve = sb("ve", [P, 2])
        rs = sb("rs", [P, 2])
        XN = sb("XN", [P, 2, D])
        XT = sb("XT", [P, KC, T])
        QT = sb("QT", [P, KC, T])
        KT = sb("KT", [P, KC, T])
        ks = sb("ks", [P, KC])
        KZ = sb("KZ", [P, KC, T])
        QA = sb("QA", [P, QW])
        QB = sb("QB", [P, QW])
        VZ = [sb(f"VZ{n}", [P, 2, NH * 2 * HD]) for n in range(RING)]
        S = [sb(f"S{n}", [P, NT, T]) for n in range(2)]
        E = [sb(f"E{n}", [P, NT, T]) for n in range(2)]
        PR = sb("PR", [P, NT, T])
        X = [sb(f"X{n}", [P, T]) for n in range(5)]
        W = sb("W", [P, T])
        W8 = sb("W8", [P, 8])
        WL = sb("WL", [P, 8])
        JK = sb("JK", [P, 8, T])
        sq, sg, g0, nt0, nt1, nt2 = [sb(f"thr{n}", [P, NT]) for n in range(6)]
        t2 = [sb(f"t2{n}", [P, NT]) for n in range(2)]
        c0, c1, c2, e0, d0, e1, dc, qq, pp, mm, nn, rp, jx = [sb(f"cnt{n}", [P, NT]) for n in range(13)]
        HALVES = sb("HALVES", [P, NT])
        MINUS1 = sb("MINUS1", [P, NT])
        M16 = sb("M16", [P, NT, WIN])
        IOTA = sb("IOTA", [P, NT, WIN])
        EQ = sb("EQ", [P, NT, WIN])
        A1 = sb("A1", [P, NT, WIN])
        A2 = sb("A2", [P, NT, WIN - 1])
        TV = sb("TV", [P, NT])
        NV = sb("NV", [P, NT])
        GT = sb("GT", [P, NT])
        OK = sb("OK", [P, NT])
        OKV = sb("OKV", [P, NT])
        okc = sb("okc", [P, 1])
        VALID = sb("VALID", [P, NT])
        flag = sb("flag", [1, 1], i32)
        mx = sb("mx", [P, NT])
        nb = sb("nb", [P, NT])
        PTT = sb("PTT", [P, NT * P])
        PTI = sb("PTI", [P, NT * P])
        RD = sb("RD", [P, KC, T])
        CT = sb("CT", [P, KC, T])
        HM = sb("HM", [P, 2, D])
        bst = sb("bst", [P, 2, 6])
        bmv = sb("bmv", [P, 2, 2])
        bve = sb("bve", [P, 2])
        brs = sb("brs", [P, 2])
        X2 = [sb(f"X2{n}", [P, 2, XW]) for n in range(2)]
        X2T = sb("X2T", [P, KC, T])
        TH = sb("TH", [FC, NF, T])
        HT = sb("HT", [FC, NF, T])
        OT = [sb(f"OT{n}", [P, 2, D]) for n in range(2)]
        L8 = sb("L8", [P, 2, 8])
        nl = sb("nl", [P, 2])
        MR = sb("MR", [P, 2, NE])
        MK = sb("MK", [P, 2, NE])
        EX = sb("EX", [P, 2, NE])
        e8 = sb("e8", [P, 2, 8])
        s8 = sb("s8", [P, 2])
        r8 = sb("r8", [P, 2])
        PO = sb("PO", [P, 2, NE])
        KEEP = sb("KEEP", [P, 2, NE])
        carry = sb("carry", [P, NE])
        N8 = sb("N8", [P, 2, 8])
        SLOT = [sb(f"SLOT{n}", [P, 2, 8], u32) for n in range(2)]
        tokf = sb("tokf", [P, 2])
        TOKI = [sb(f"TOKI{n}", [P, 2], i32) for n in range(2)]

        ids_i = sb("ids_i", [NE, CAP], i32)
        ids_f = sb("ids_f", [NE, CAP])
        ids_t = sb("ids_t", [CAP, NE], u32)
        IX = [sb(f"IX{n}", [CAP, 1], u32) for n in range(EB)]
        taken = {}

        def reuse(area, shape):
            at = taken.get(area.name, 0)
            size = 1
            for n in shape[1:]:
                size *= n
            taken[area.name] = at + size
            flat = area[0:shape[0], :, :].rearrange("p t n -> p (t n)")[:, at:at + size]
            return flat if len(shape) == 2 else flat.rearrange("p (k n) -> p k n", k=shape[1])

        WG = [reuse(S[0], [P, KC, FF]) for n in range(EB)]
        WU = [reuse(S[0], [P, KC, FF]) for n in range(EB)]
        WD = [reuse(S[1], [FC, NF, D]) for n in range(EB)]
        XE = reuse(S[1], [P, KC, CAP])
        TG = reuse(S[1], [FC, NF, CAP])
        HE = reuse(S[1], [FC, NF, CAP])
        XG = [reuse(E[0], [CAP, XW]) for n in range(EB)]
        Y = [reuse(E[0], [CAP, D]) for n in range(EB)]
        TE = reuse(E[0], [FC, NF, CAP])

        banks = [ctx.enter_context(nc.psum_tensor(f"bank{n}", [P, 512], fp32)) for n in range(8)]
        bS, bT, bI, bF, bX, bY = banks[0:3], banks[3], banks[4], banks[5], banks[6], banks[7]

        def chunks(bank, n, w):
            return bank[:, 0:n * w].rearrange("p (c n) -> p c n", c=n)

        s_const, s_wts, s_setup = sem("s_const"), sem("s_wts"), sem("s_setup")
        s_bo, s_z, s_bv = sem("s_bo"), sem("s_z"), sem("s_bv")
        s_patch, s_txt = [sem(f"s_patch{n}") for n in range(2)], [sem(f"s_txt{n}") for n in range(RING)]
        s_fp, FP = sem("s_fp"), 5
        s_fd, FD = sem("s_fd"), 9
        s_fa, FA = sem("s_fa"), 6
        s_fg, FG = sem("s_fg"), 10
        s_diag, DG = sem("s_diag"), 16 * NH
        s_score = sem("s_score")
        s_take = sem("s_take")
        s_exp, EX_N = sem("s_exp"), NG * (2 * GROUP + 1)
        s_cnt, CN = sem("s_cnt"), 3 * NT
        s_up, UP = sem("s_up"), 24
        s_place = sem("s_place")
        s_pick, PK_N = sem("s_pick"), 4 * NT
        s_sel, SEL = sem("s_sel"), 9
        s_flag = sem("s_flag")
        s_slow = sem("s_slow")
        s_prob = sem("s_prob")
        s_tr, TR_N = sem("s_tr"), NT
        s_trc, TRC_N = sem("s_trc"), 2 * -(-NT // 4)
        s_bp, BP = sem("s_bp"), 9
        s_bd, BD = sem("s_bd"), 28
        s_ba, BA = sem("s_ba"), 7
        s_bg, BG = sem("s_bg"), 2
        s_tok = sem("s_tok")
        s_xrow, s_out = [[sem(f"{what}{n}") for n in range(2)] for what in ("s_xrow", "s_out")]
        s_slot, SL = [sem(f"s_slot{n}") for n in range(2)], 16 * 16
        s_zero, s_empty = sem("s_zero"), sem("s_empty")
        s_gate_d, s_gate_g, s_gate_s = sem("s_gate_d"), sem("s_gate_g"), sem("s_gate_s")
        s_ids, s_idt, s_idp = sem("s_ids"), sem("s_idt"), sem("s_idp")
        s_ew, s_xg = [[sem(f"{what}{n}") for n in range(EB)] for what in ("s_ew", "s_xg")]
        s_ix, s_ep, s_ea, s_ed, s_add = sem("s_ix"), sem("s_ep"), sem("s_ea"), sem("s_ed"), sem("s_add")

        block = ctx.enter_context(nc.Block())

        def batches(eng, body):
            loops = max(0, (n_batch - 2 - FIRST) // RING)
            for i in range(-1, FIRST):
                body(i, i % RING)
            if loops > 1:
                with eng.Fori(0, loops) as n:
                    for u in range(RING):
                        body(n * RING + FIRST + u, (FIRST + u) % RING)
            else:
                loops = 0
            for i in range(FIRST + RING * loops, n_batch + 3):
                body(i, i % RING)

        def experts(eng, body):
            for k in range(EB):
                body(k, k)
            with eng.Fori(1, NE // EB - 1) as n:
                for k in range(EB):
                    body(n * EB + k, k)
            for k in range(EB):
                body(NE - EB + k, k)

        def stored(eng):
            eng.wait_ge(s_zero, 32)
            for s in s_xrow, s_out:
                for n in range(2):
                    eng.wait_ge(s[n], 32 * len(range(n, n_batch, 2)))

        def of_ring(b, r, ring, n):
            return (n // ring) * (b - r) + n

        def known(i):
            return isinstance(i, int)

        def has(i):
            return not known(i) or 0 <= i < n_batch

        def ahead(eng, s, value, batch):
            if not known(batch) or batch >= 0:
                eng.wait_ge(s, value)

        def parts(c):
            return (P, IMG, T) if c == 0 else (IMG, 0, IMG)

        @block.sync
        def _(sp):
            for dst, src in ((WT[:, :, :], w_tok.rearrange("(k p) n -> p k n", p=P)),
                             (WQ[:, :, :], w_qkv.rearrange("(k p) n -> p k n", p=P)),
                             (WO[:, :, :], w_out.rearrange("(k p) n -> p k n", p=P)),
                             (WR[:, :, :], router.rearrange("(k p) n -> p k n", p=P)),
                             (WSG[:, :, :], ws_gate_up.rearrange("(k p) n -> p k n", p=P)),
                             (WSD[:, :, :], ws_down.rearrange("(k p) n -> p k n", p=FC)),
                             (POSB[:, :], pos[0, :, :]),
                             (BT[0:1, :], cls[0, :, :]),
                             (BT[1:IMG, :], b_tok.partition_broadcast(IMG - 1)),
                             (GAM[:, :], gamma.partition_broadcast(IMG)),
                             (BET[:, :], beta.partition_broadcast(IMG)),
                             (BO[:, :], b_out.partition_broadcast(P)),
                             (BQ[:, :], b_q), (BK[:, :], b_k), (BV[:, :], b_v)):
                sp.dma_start(dst, src).then_inc(s_wts, 16)
            sp.wait_ge(s_z, 2)
            sp.dma_start(x_rows[tokens:tokens + CAP, :], ZR[:, :]).then_inc(s_zero, 16)
            sp.dma_start(out[tokens:tokens + CAP, :], ZR[:, 0:D]).then_inc(s_zero, 16)
            sp.wait_ge(s_setup, 3)

            def gated():
                sp.sem_inc(s_gate_s, 1)

            def load(b, r):
                ahead(sp, s_fp, FP * (b - 2) + 1, b - 2 if known(b) else b)
                gated()
                sp.dma_start(PT[r % 2][:, :, 1:IMG], patches[bass.ds(b, 1), :, :, :].rearrange("a p k n -> p (a k) n"))\
                    .then_inc(s_patch[r % 2], 16)
                ahead(sp, s_bd, BD * (b - RING) + 3, b - RING if known(b) else b)
                gated()
                sp.dma_start(H[r][:, 0, :], txt[bass.ds(b, 1), :, :].rearrange("a p n -> p (a n)")).then_inc(s_txt[r], 16)

            def diagonal(b):
                sp.wait_ge(s_fa, FA * b + 3)
                gated()
                ahead(sp, s_score, NG * b, b - 1 if known(b) else b)
                gated()
                for h in range(NH):
                    dst, at = (QA, T * h) if h < HALF else (QB, LEAD + T * (h - HALF))
                    p = HD * (h % HALF)
                    sp.dma_start(dst[p:p + HD, at:at + T], QT[p:p + HD, h // HALF, :]).then_inc(s_diag, 16)

            def store(b, r):
                sp.wait_ge(s_bd, BD * b + 12)
                gated()
                sp.dma_start(out[bass.ds(b * T + IMG, TXT), :], OT[r % 2][:, 0, :]).then_inc(s_out[r % 2], 16)
                sp.dma_start(out[bass.ds(b * T, IMG), :], OT[r % 2][0:IMG, 1, :]).then_inc(s_out[r % 2], 16)
                sp.wait_ge(s_bd, BD * b + 20)
                gated()
                sp.dma_start(x_rows[bass.ds(b * T + IMG, TXT), :], X2[r % 2][:, 0, :]).then_inc(s_xrow[r % 2], 16)
                sp.dma_start(x_rows[bass.ds(b * T, IMG), :], X2[r % 2][0:IMG, 1, :]).then_inc(s_xrow[r % 2], 16)

            def iteration(i, r):
                if known(i) and i == -1:
                    load(0, 0)
                if has(i - 3):
                    store(i - 3, (r - 3) % RING)
                if has(i + 2):
                    load(i + 2, (r + 2) % RING)
                if has(i + 1):
                    diagonal(i + 1)

            def load_expert(e, k):
                if not known(e) or e >= EB:
                    sp.wait_ge(s_ep, 4 * (e - EB + 1))
                gated()
                for w, src, p in ((WG, w_gate, P), (WU, w_up, P), (WD, w_down, FC)):
                    sp.dma_start(w[k][:, :, :], src[bass.ds(e, 1), :, :].rearrange("a (k p) n -> p (a k) n", p=p))\
                        .then_inc(s_ew[k], 16)

            batches(sp, iteration)
            sp.wait_ge(s_cnt, CN * n_batch)
            sp.wait_ge(s_prob, NT * n_batch)
            for e in range(EB):
                load_expert(e, e)
            with sp.Fori(1, NE // EB) as n:
                for k in range(EB):
                    load_expert(n * EB + k, k)
            stored(sp)

        @block.gpsimd
        def _(pool):
            done = [0]

            def const(ins):
                done[0] += 1
                ins.then_inc(s_const, 1)

            const(pool.memset(IDENT[:, :], 0.0))
            const(pool.memset(TRI[:, :], 1.0))
            const(pool.memset(ONES[:, :], 1.0))
            const(pool.memset(ONESZ[:, :, :], 0.0))
            const(pool.memset(PAD[:, :, :], 1.0))
            const(pool.memset(PW[:, :], -0.5))
            const(pool.iota(CST[:, :], [[-CAP, NE]], base=FAR, channel_multiplier=0, allow_small_or_imprecise_dtypes=True))
            const(pool.iota(tokf[:, 0:1], [[0, 1]], base=IMG, channel_multiplier=1, allow_small_or_imprecise_dtypes=True))
            const(pool.iota(tokf[:, 1:2], [[0, 1]], base=0, channel_multiplier=1, allow_small_or_imprecise_dtypes=True))
            pool.wait_ge(s_const, done[0])
            const(pool.affine_select(out=IDENT[:, :], in_=IDENT[:, :], compare_op=ALU.not_equal, fill=1.0, base=0,
                                     pattern=[[-1, P]], channel_multiplier=1))
            const(pool.affine_select(out=TRI[:, :], in_=TRI[:, :], compare_op=ALU.is_gt, fill=0.0, base=0,
                                     pattern=[[1, P]], channel_multiplier=-1))
            const(pool.affine_select(out=PAD[:, 1, :], in_=PAD[:, 1, :], compare_op=ALU.is_gt, fill=0.0, base=IMG,
                                     pattern=[[0, NE]], channel_multiplier=-1))
            const(pool.memset(ONESZ[:, 0, 0:HD], 1.0))
            const(pool.memset(ONESZ[:, 1, HD:2 * HD], 1.0))
            pool.memset(ZR[:, :], 0.0).then_inc(s_z, 1)
            ids0 = ids_i[:, :]
            pool.iota(ids0, [[1, CAP]], base=tokens, channel_multiplier=0).then_inc(s_z, 1)
            for t in (QA, QB, PTI):
                const(pool.memset(t[:, :], 0.0))
            for t in VZ + H:
                const(pool.memset(t[:, :, :], 0.0))
            for t in PT:
                const(pool.memset(t[:, :, 0:1], 0.0))
            const(pool.memset(carry[:, :], 0.0))
            const(pool.memset(WL[:, :], LOW))
            const(pool.memset(HALVES[:, :], 0.5))
            const(pool.memset(MINUS1[:, :], -1.0))
            const(pool.memset(VALID[:, :], 1.0))
            const(pool.iota(IOTA[:, :, :], [[0, NT], [1, WIN]], base=0, channel_multiplier=0,
                            allow_small_or_imprecise_dtypes=True))
            pool.wait_ge(s_const, done[0])
            const(pool.affine_select(out=VALID[:, NT - 1:NT], in_=VALID[:, NT - 1:NT], compare_op=ALU.is_gt, fill=0.0,
                                     base=ROWS - (NT - 1) * P, pattern=[[0, 1]], channel_multiplier=-1))
            const(pool.memset(mv[:, :, :], 1.0))
            pool.wait_ge(s_const, done[0])
            pool.wait_ge(s_z, 2)
            pool.dma_start(slot_token.rearrange("(e c) n -> e (c n)", e=NE), ids0).then_inc(s_empty, 16)
            pool.wait_ge(s_empty, 16)
            pool.sem_inc(s_setup, 1)
            pool.wait_ge(s_bo, 3)
            pool.sem_inc(s_setup, 1)
            pool.wait_ge(s_wts, 16 * 15)
            pool.sem_inc(s_setup, 1)

            def gated():
                pool.sem_inc(s_gate_g, 1)

            def front_scale(b):
                pool.wait_ge(s_fd, FD * b + 3)
                gated()
                pool.tensor_scalar(ve[0:IMG, 0:1], mv[0:IMG, 0, 1:2], EPS, None, ALU.add).then_inc(s_fg, 1)
                pool.wait_ge(s_fg, FG * b + 1)
                pool.tensor_tensor(rs[0:IMG, 0:1], ve[0:IMG, 0:1], PW[0:IMG, 0:1], ALU.pow).then_inc(s_fg, 1)

            def front_affine(b, r):
                pool.wait_ge(s_fd, FD * b + 4)
                pool.tensor_tensor(TK[:, :], TK[:, :], GAM[:, :], ALU.mult).then_inc(s_fg, 1)
                ahead(pool, s_bd, BD * (b - RING) + 3, b - RING if known(b) else b)
                pool.wait_ge(s_fg, FG * b + 3)
                pool.tensor_tensor(H[r][0:IMG, 1, :], TK[:, :], BET[:, :], ALU.add).then_inc(s_fg, 1)

            def front_scale2(b):
                pool.wait_ge(s_fd, FD * b + 7)
                gated()
                pool.tensor_scalar(ve[:, :], mv[:, :, 1], EPS, None, ALU.add).then_inc(s_fg, 1)
                pool.wait_ge(s_fg, FG * b + 5)
                pool.tensor_tensor(rs[:, :], ve[:, :], PW[:, :], ALU.pow).then_inc(s_fg, 1)

            def front_bias(b, r):
                pool.wait_ge(s_fd, FD * b + 9)
                pool.tensor_tensor(H[r][:, 0, :], H[r][:, 0, :], BO[:, :], ALU.add).then_inc(s_fg, 1)
                pool.tensor_tensor(H[r][0:IMG, 1, :], H[r][0:IMG, 1, :], BO[0:IMG, :], ALU.add).then_inc(s_fg, 1)

            def front_center(b):
                pool.wait_ge(s_fa, FA * b + 5)
                ahead(pool, s_score, NG * b, b - 1 if known(b) else b)
                gated()
                pool.tensor_scalar(ks[:, :], ks[:, :], -1.0 / T, None, ALU.mult).then_inc(s_fg, 1)
                pool.wait_ge(s_fg, FG * b + 9)
                gated()
                for k in range(KC):
                    last = pool.tensor_scalar(KZ[:, k, :], KT[:, k, :], ks[:, k:k + 1], 1.0, ALU.add, ALU.mult)
                last.then_inc(s_fg, 1)

            def gated_step(i, k, *waits):
                if k:
                    pool.wait_ge(s_up, UP * i + k)
                for s, v in waits:
                    pool.wait_ge(s, v)
                gated()

            def guess(i, half):
                lo, hi, n = (0, AHEAD, 0) if half == 0 else (AHEAD, NT, 4)
                gated_step(i, n, (s_exp, EX_N * i + (2 * GROUP + 1) * hi // GROUP - GROUP - 1))
                pool.tensor_scalar(sg[:, lo:hi], sq[:, lo:hi], 1.0 / T, 1e-30, ALU.mult, ALU.add).then_inc(s_up, 1)
                gated_step(i, n + 1)
                pool.tensor_tensor(sg[:, lo:hi], sg[:, lo:hi], HALVES[:, lo:hi], ALU.pow).then_inc(s_up, 1)
                gated_step(i, n + 2)
                pool.tensor_scalar(nt0[:, lo:hi], sg[:, lo:hi], -GUESS, 1.0, ALU.mult, ALU.mult).then_inc(s_up, 1)
                pool.tensor_scalar(g0[:, lo:hi], sg[:, lo:hi], SLOPE, 1.0, ALU.mult, ALU.mult).then_inc(s_up, 1)

            def refine(i):
                gated_step(i, 8, (s_cnt, CN * i + NT))
                pool.tensor_scalar(e0[:, :], c0[:, :], 0.5, T / 2 - AIM, ALU.mult, ALU.add).then_inc(s_up, 1)
                pool.wait_ge(s_up, UP * i + 9)
                pool.tensor_tensor(d0[:, :], e0[:, :], g0[:, :], ALU.mult).then_inc(s_up, 1)
                pool.wait_ge(s_up, UP * i + 10)
                pool.tensor_tensor(nt1[:, :], nt0[:, :], d0[:, :], ALU.subtract).then_inc(s_up, 1)

            def refine2(i, r):
                gated_step(i, 0, (s_cnt, CN * i + 2 * NT))
                pool.tensor_scalar(e1[:, :], c1[:, :], 0.5, T / 2 - AIM, ALU.mult, ALU.add).then_inc(s_up, 1)
                pool.tensor_tensor(dc[:, :], c0[:, :], c1[:, :], ALU.subtract).then_inc(s_up, 1)
                gated_step(i, 13)
                pool.tensor_tensor(qq[:, :], e1[:, :], e1[:, :], ALU.mult).then_inc(s_up, 1)
                pool.tensor_tensor(pp[:, :], dc[:, :], dc[:, :], ALU.mult).then_inc(s_up, 1)
                gated_step(i, 15)
                pool.tensor_scalar(qq[:, :], qq[:, :], NEAR, 2.0, ALU.is_gt, ALU.mult).then_inc(s_up, 1)
                pool.tensor_scalar(pp[:, :], pp[:, :], 1.0, None, ALU.max).then_inc(s_up, 1)
                gated_step(i, 17)
                pool.tensor_tensor(mm[:, :], e1[:, :], qq[:, :], ALU.mult).then_inc(s_up, 1)
                pool.tensor_tensor(rp[:, :], pp[:, :], MINUS1[:, :], ALU.pow).then_inc(s_up, 1)
                pool.tensor_tensor(nn[:, :], d0[:, :], dc[:, :], ALU.mult).then_inc(s_up, 1)
                gated_step(i, 20)
                pool.tensor_tensor(mm[:, :], mm[:, :], nn[:, :], ALU.mult).then_inc(s_up, 1)
                gated_step(i, 21)
                pool.tensor_tensor(mm[:, :], mm[:, :], rp[:, :], ALU.mult).then_inc(s_up, 1)
                gated_step(i, 22)
                pool.tensor_tensor(nt2[:, :], nt1[:, :], mm[:, :], ALU.subtract).then_inc(s_up, 1)
                gated_step(i, 23)
                pool.tensor_scalar(t2[r % 2][:, :], nt2[:, :], -1.0, 1.0, ALU.mult, ALU.mult).then_inc(s_up, 1)

            def place(i):
                ahead(pool, s_sel, SEL * i, i - 1 if known(i) else i)
                pool.wait_ge(s_cnt, CN * (i + 1))
                gated()
                pool.tensor_scalar(jx[:, :], c2[:, :], -0.5, TOPK - 1 - T / 2, ALU.mult, ALU.add).then_inc(s_place, 1)

            def back_scale(b):
                pool.wait_ge(s_bd, BD * b + 7)
                gated()
                pool.tensor_scalar(bve[:, :], bmv[:, :, 1], EPS, None, ALU.add).then_inc(s_bg, 1)
                pool.wait_ge(s_bg, BG * b + 1)
                pool.tensor_tensor(brs[:, :], bve[:, :], PW[:, :], ALU.pow).then_inc(s_bg, 1)

            def back_tokens(b, r):
                ahead(pool, s_slot[r % 2], of_ring(b - 2, r % 2, 2, SL), b - 2 if known(b) else b)
                ahead(pool, s_tok, 2 * b, b - 1 if known(b) else b)
                gated()
                pool.tensor_copy(TOKI[r % 2][:, :], tokf[:, :]).then_inc(s_tok, 1)
                pool.wait_ge(s_tok, 2 * b + 1)
                gated()
                pool.tensor_scalar(tokf[:, :], tokf[:, :], float(T), None, ALU.add).then_inc(s_tok, 1)

            def back_slots(b, r, c):
                pool.wait_ge(s_bd, BD * b + 28)
                gated()
                n = parts(c)[0]
                for k in range(8):
                    pool.indirect_dma_start(slot_token, bass.IndirectOffsetOnAxis(SLOT[r % 2][0:n, c, k:k + 1], 0),
                                            TOKI[r % 2][0:n, c:c + 1], None, bounds_check=SLOTS - 1,
                                            oob_is_err=False).then_inc(s_slot[r % 2], 16)

            def iteration(i, r):
                f, b, s = has(i + 1), has(i - 2), has(i - 3)
                if f:
                    front_scale(i + 1)
                    front_affine(i + 1, (r + 1) % RING)
                    front_scale2(i + 1)
                    front_bias(i + 1, (r + 1) % RING)
                if has(i):
                    guess(i, 0)
                    guess(i, 1)
                if has(i - 1):
                    place(i - 1)
                if s:
                    back_tokens(i - 3, (r - 3) % RING)
                    back_slots(i - 3, (r - 3) % RING, 1)
                if has(i):
                    refine(i)
                if f:
                    front_center(i + 1)
                if s:
                    back_slots(i - 3, (r - 3) % RING, 0)
                if b:
                    back_scale(i - 2)
                if has(i):
                    refine2(i, r)

            batches(pool, iteration)
            for n in range(2):
                pool.wait_ge(s_slot[n], SL * len(range(n, n_batch, 2)))
            pool.dma_start(ids_i[:, :], slot_token.rearrange("(e c) n -> e (c n)", e=NE)).then_inc(s_ids, 16)

            def gather(e, k):
                pool.wait_ge(s_ix, e + 1)
                gated()
                pool.indirect_dma_start(XG[k][:, :], None, x_rows, bass.IndirectOffsetOnAxis(IX[k][:, :], 0))\
                    .then_inc(s_xg[k], 16)

            def add(e, k):
                pool.wait_ge(s_ed, 3 * e + 3)
                ahead(pool, s_add, 16 * e, e)
                gated()
                pool.indirect_dma_start(out, bass.IndirectOffsetOnAxis(IX[k][:, :], 0), Y[k][:, :], None,
                                        compute_op=ALU.add).then_inc(s_add, 16)

            stored(pool)
            def expert(e, k):
                if not known(e) or e + 2 < NE:
                    gather(e + 2, (k + 2) % EB)
                add(e, k)

            gather(0, 0)
            gather(1, 1)
            experts(pool, expert)
            pool.wait_ge(s_add, 16 * NE)

        @block.scalar
        def _(act):
            act.wait_ge(s_setup, 3)

            def front_xt(b):
                act.wait_ge(s_fp, FP * b + 2)
                act.activation(XT[:, :, :], chunks(bF, KC, T), ACT.Copy).then_inc(s_fa, 1)

            def front_q(b):
                act.wait_ge(s_fp, FP * b + 3)
                ahead(act, s_diag, DG * b, b - 1 if known(b) else b)
                for k in range(KC):
                    act.activation(QT[:, k, :], chunks(bF, KC, T)[:, k, :], ACT.Identity, bias=BQ[:, k:k + 1]).then_inc(s_fa, 1)

            def front_k(b):
                act.wait_ge(s_fp, FP * b + 4)
                ahead(act, s_fg, FG * b, b - 1 if known(b) else b)
                for k in range(KC):
                    act.activation(KT[:, k, :], chunks(bF, KC, T)[:, k, :], ACT.Identity, bias=BK[:, k:k + 1],
                                   accum_out=ks[:, k:k + 1]).then_inc(s_fa, 1)

            def front_v(b, r):
                act.wait_ge(s_fp, FP * b + 5)
                ahead(act, s_bp, BP * (b - RING) + 1, b - RING if known(b) else b)
                for c in range(2):
                    n = parts(c)[0]
                    v = chunks(bF, 2, D)[0:n, c, :].rearrange("p (g a d) -> p g a d", g=HALF, a=2)
                    z = VZ[r][0:n, c, :].rearrange("p (g x) -> p g x", g=HALF)
                    for a in range(2):
                        last = act.activation(z[:, :, 3 * HD * a:3 * HD * a + HD], v[:, :, a, :], ACT.Copy)
                last.then_inc(s_fa, 1)

            def exps(i, r, g):
                n = EX_N * i + (2 * GROUP + 1) * g
                tiles = range(GROUP * g, GROUP * (g + 1))
                act.wait_ge(s_take, NT * i + GROUP * (g + 1))
                if g == 0:
                    ahead(act, s_up, UP * (i - 1) + 5, i - 1 if known(i) else i)
                    ahead(act, s_prob, NT * (i - 1), i - 2 if known(i) else i)
                for t in tiles:
                    act.activation(E[r % 2][:, t, :], chunks(bS[g % 3], GROUP, T)[:, t % GROUP, :], ACT.Square,
                                   accum_out=sq[:, t:t + 1]).then_inc(s_exp, 1)
                act.activation(nb[:, GROUP * g:GROUP * (g + 1)], mx[:, GROUP * g:GROUP * (g + 1)], ACT.Copy,
                               scale=-SCALE).then_inc(s_exp, 1)
                act.wait_ge(s_exp, n + GROUP + 1)
                for t in tiles:
                    act.activation(E[r % 2][:, t, :], chunks(bS[g % 3], GROUP, T)[:, t % GROUP, :], ACT.Exp,
                                   bias=nb[:, t:t + 1], scale=SCALE).then_inc(s_exp, 1)

            def count(i, r, n, tiles=range(NT)):
                for t in tiles:
                    if t == 0:
                        act.wait_ge(s_up, UP * i + (3, 11, 23)[n])
                    if t == 0 and n == 0:
                        act.wait_ge(s_take, NT * i + AHEAD)
                    if t == 0 and n == 2:
                        ahead(act, s_place, i, i - 1 if known(i) else i)
                    if t == AHEAD and n == 0:
                        act.wait_ge(s_up, UP * i + 7)
                        act.wait_ge(s_take, NT * (i + 1))
                    if t % 4 == 0 and (n or t or not known(i) or i):
                        act.wait_ge(s_cnt, CN * i + NT * n + max(t - 4, 0))
                    act.activation(JK[:, t % 8, :], S[r % 2][:, t, :], ACT.Sign, bias=(nt0, nt1, nt2)[n][:, t:t + 1],
                                   accum_out=(c0, c1, c2)[n][:, t:t + 1]).then_inc(s_cnt, 1)

            def transposed(i, n):
                w = min(4, NT - 4 * n) * P
                act.wait_ge(s_tr, TR_N * i + min(4 * n + 4, NT))
                if n == 0:
                    ahead(act, s_bp, BP * (i - 1) + 2, i - 1 if known(i) else i)
                act.activation(PTT[:, 4 * P * n:4 * P * n + w], bT[:, 0:w], ACT.Copy).then_inc(s_trc, 1)
                act.activation(PTI[0:IMG, 4 * P * n:4 * P * n + w], bI[0:IMG, 0:w], ACT.Copy).then_inc(s_trc, 1)

            def back_xt(b):
                act.wait_ge(s_bp, BP * b + 4)
                act.activation(X2T[:, :, :], chunks(bY, KC, T), ACT.Copy).then_inc(s_ba, 1)

            def back_tanh(b):
                act.wait_ge(s_bp, BP * b + 5)
                act.activation(TH[:, :, :], chunks(bX, NF, T)[0:FC], ACT.Tanh, scale=0.5).then_inc(s_ba, 1)

            def back_weights(b):
                act.wait_ge(s_bd, BD * b + 16)
                act.activation(nl[:, :], L8[:, :, 0], ACT.Copy, scale=-1.0).then_inc(s_ba, 1)
                act.wait_ge(s_ba, BA * b + 3)
                for c in range(2):
                    act.activation(EX[:, c, :], chunks(bY, 2, NE)[:, c, :], ACT.Exp, bias=nl[:, c:c + 1]).then_inc(s_ba, 1)
                for c in range(2):
                    act.activation(e8[:, c, :], L8[:, c, :], ACT.Exp, bias=nl[:, c:c + 1],
                                   accum_out=s8[:, c:c + 1]).then_inc(s_ba, 1)

            def iteration(i, r):
                f, b = has(i + 1), has(i - 2)
                for g in range(NG):
                    if has(i):
                        exps(i, r, g)
                    if b and g < TRC_N // 2:
                        transposed(i - 2, g)
                    if has(i - 1):
                        count(i - 1, (r - 1) % RING, 2, range(GROUP * g, GROUP * (g + 1)))
                    if has(i - 3) and g == 1:
                        back_tanh(i - 3)
                    if has(i - 3) and g == 4:
                        back_weights(i - 3)
                if f:
                    front_xt(i + 1)
                    front_q(i + 1)
                if has(i):
                    count(i, r, 0)
                if f:
                    front_k(i + 1)
                    front_v(i + 1, (r + 1) % RING)
                if has(i):
                    count(i, r, 1)
                if b:
                    back_xt(i - 2)

            batches(act, iteration)

            def expert(e, k):
                act.wait_ge(s_ep, 4 * e + 1)
                act.activation(XE[:, :, :], chunks(bT, KC, P), ACT.Copy).then_inc(s_ea, 1)
                act.wait_ge(s_ep, 4 * e + 2)
                act.activation(TE[:, :, :], chunks(bX, NF, P)[0:FC], ACT.Tanh, scale=0.5).then_inc(s_ea, 1)

            experts(act, expert)

        @block.vector
        def _(dve):
            dve.wait_ge(s_wts, 16 * 15)
            dve.tensor_tensor(POSB[:, :], POSB[:, :], BT[:, :], ALU.add).then_inc(s_bo, 1)
            dve.tensor_copy(BVR[:, :, :], BV[:, :].rearrange("p (k a) -> p k a", a=1).to_broadcast([P, KC, P])).then_inc(s_bo, 1)
            dve.wait_ge(s_bv, 1)
            dve.tensor_tensor(BO[:, :], BO[:, :], bX[:, 0:D], ALU.add).then_inc(s_bo, 1)
            dve.wait_ge(s_setup, 3)

            def gated():
                dve.sem_inc(s_gate_d, 1)

            def step(s, n, b):
                def upto(k):
                    dve.wait_ge(s, n * b + k)
                return upto

            def front_embed(b):
                seen = step(s_fd, FD, b)
                dve.wait_ge(s_fp, FP * b + 1)
                ahead(dve, s_fg, FG * b, b - 1 if known(b) else b)
                dve.tensor_tensor(TK[:, :], bF[0:IMG, 0:D], POSB[:, :], ALU.add).then_inc(s_fd, 1)
                seen(1)
                dve.bn_stats(st[0:IMG, 0, :], TK[:, :]).then_inc(s_fd, 1)
                seen(2)
                gated()
                dve.bn_aggr(mv[0:IMG, 0, :], st[0:IMG, 0, :]).then_inc(s_fd, 1)

            def front_embed2(b):
                dve.wait_ge(s_fg, FG * b + 2)
                dve.tensor_scalar(TK[:, :], TK[:, :], mv[0:IMG, 0, 0:1], rs[0:IMG, 0:1], ALU.subtract, ALU.mult).then_inc(s_fd, 1)

            def front_norm(b, r):
                dve.wait_ge(s_txt[r], of_ring(b, r, RING, 16))
                dve.wait_ge(s_fd, FD * b + 4)
                dve.bn_stats(st[:, 0, :], H[r][:, 0, :]).then_inc(s_fd, 1)
                dve.wait_ge(s_fg, FG * b + 4)
                dve.bn_stats(st[0:IMG, 1, :], H[r][0:IMG, 1, :]).then_inc(s_fd, 1)
                dve.wait_ge(s_fd, FD * b + 6)
                gated()
                dve.bn_aggr(mv[:, 0, :], st[:, 0, :])
                dve.bn_aggr(mv[0:IMG, 1, :], st[0:IMG, 1, :]).then_inc(s_fd, 1)

            def front_norm2(b, r):
                dve.wait_ge(s_fg, FG * b + 6)
                ahead(dve, s_fp, FP * (b - 1) + 2, b - 1 if known(b) else b)
                dve.tensor_scalar(XN[:, 0, :], H[r][:, 0, :], mv[:, 0, 0:1], rs[:, 0:1], ALU.subtract, ALU.mult).then_inc(s_fd, 1)
                dve.tensor_scalar(XN[0:IMG, 1, :], H[r][0:IMG, 1, :], mv[0:IMG, 1, 0:1], rs[0:IMG, 1:2],
                                  ALU.subtract, ALU.mult).then_inc(s_fd, 1)

            def take(i, r, g):
                if g == 0:
                    ahead(dve, s_exp, EX_N * i, i - 1 if known(i) else i)
                    ahead(dve, s_cnt, CN * (i - 1), i - 2 if known(i) else i)
                    ahead(dve, s_prob, NT * (i - 1), i - 2 if known(i) else i)
                dve.wait_ge(s_score, NG * i + g + 1)
                for t in range(GROUP * g, GROUP * (g + 1)):
                    dve.tensor_scalar(S[r % 2][:, t, :], chunks(bS[g % 3], GROUP, T)[:, t % GROUP, :], 1.0, None,
                                      ALU.mult, ALU.max, accum_out=mx[:, t:t + 1]).then_inc(s_take, 1)

            def issued(n):
                return sum(min(max(n - k, 0), NT) for k in range(4))

            def pick(i, r, n):
                if n == 0:
                    dve.wait_ge(s_up, UP * i + 24)
                    ahead(dve, s_sel, SEL * i, i - 1 if known(i) else i)
                else:
                    dve.wait_ge(s_pick, PK_N * i + issued(n) - (1 if n > 3 else 0))
                if n < NT:
                    dve.scalar_tensor_tensor(X[n % 5][:, :], S[r % 2][:, n, :], t2[r % 2][:, n:n + 1], S[r % 2][:, n, :],
                                             ALU.is_lt, ALU.mult).then_inc(s_pick, 1)
                else:
                    gated()
                if 1 <= n <= NT:
                    t = n - 1
                    dve.max(M16[:, t, 0:8], X[t % 5][:, :]).then_inc(s_pick, 1)
                if 2 <= n <= NT + 1:
                    t = n - 2
                    dve.match_replace(X[t % 5][:, :], M16[:, t, 0:8], X[t % 5][:, :], LOW).then_inc(s_pick, 1)
                if 3 <= n:
                    t = n - 3
                    dve.max(M16[:, t, 8:WIN], X[t % 5][:, :]).then_inc(s_pick, 1)

            def threshold(i):
                seen = step(s_sel, SEL, i)
                place = jx[:, :].rearrange("p (n a) -> p n a", a=1).to_broadcast([P, NT, WIN])
                dve.wait_ge(s_place, i + 1)
                dve.tensor_tensor(EQ[:, :, :], IOTA[:, :, :], place, ALU.is_equal).then_inc(s_sel, 1)
                dve.wait_ge(s_pick, PK_N * (i + 1))
                seen(1)
                dve.tensor_tensor(A1[:, :, :], EQ[:, :, :], M16[:, :, :], ALU.mult).then_inc(s_sel, 1)
                dve.tensor_tensor(A2[:, :, :], EQ[:, :, 0:WIN - 1], M16[:, :, 1:WIN], ALU.mult).then_inc(s_sel, 1)
                seen(2)
                dve.tensor_reduce(TV[:, :], A1[:, :, :], AX.X, ALU.add).then_inc(s_sel, 1)
                seen(3)
                dve.tensor_reduce(NV[:, :], A2[:, :, :], AX.X, ALU.add).then_inc(s_sel, 1)
                seen(5)
                dve.tensor_tensor(GT[:, :], TV[:, :], NV[:, :], ALU.is_gt).then_inc(s_sel, 1)
                seen(6)
                dve.scalar_tensor_tensor(OK[:, :], NV[:, :], 0.0, GT[:, :], ALU.is_gt, ALU.mult).then_inc(s_sel, 1)
                seen(7)
                dve.scalar_tensor_tensor(OKV[:, :], OK[:, :], 1.0, VALID[:, :], ALU.mult, ALU.mult,
                                         accum_out=okc[:, :]).then_inc(s_sel, 1)

            unsure = ctx.enter_context(dve.register("unsure"))

            def general(i, r):
                dve.wait_ge(s_flag, i + 1)
                dve.tensor_scalar(flag[:, :], bT[0:1, 0:1], -1.0, float(ROWS), ALU.mult, ALU.add).then_inc(s_sel, 1)
                dve.wait_ge(s_sel, SEL * (i + 1))
                gated()
                dve.reg_load(unsure, flag[0:1, 0:1])
                with dve.If(dve.snap(unsure) > 0):
                    with dve.Fori(0, NT) as t:
                        dve.sem_clear(s_slow)
                        tile = S[r % 2][:, bass.ds(t, 1), :].rearrange("p a n -> p (a n)")
                        n = 0
                        dve.tensor_copy(W[:, :], tile).then_inc(s_slow, 1)
                        for rnd in range(ROUNDS + 1):
                            n += 1
                            dve.wait_ge(s_slow, n)
                            dve.max(W8[:, :], W[:, :]).then_inc(s_slow, 1)
                            n += 1
                            dve.wait_ge(s_slow, n)
                            if rnd < ROUNDS:
                                dve.match_replace(W[:, :], W8[:, :], W[:, :], LOW).then_inc(s_slow, 1)
                        dve.tensor_copy(WL[:, 0:1], W8[:, 0:1]).then_inc(s_slow, 1)
                        dve.wait_ge(s_slow, n + 1)
                        dve.match_replace(W[:, :], WL[:, :], W[:, :], LOW).then_inc(s_slow, 1)
                        dve.wait_ge(s_slow, n + 2)
                        dve.tensor_scalar(tile, W[:, :], GONE, None, ALU.is_lt).then_inc(s_slow, 1)
                        dve.wait_ge(s_slow, n + 3)
                    dve.sem_clear(s_slow)
                    dve.memset(TV[:, :], 0.5).then_inc(s_slow, 1)
                    dve.wait_ge(s_slow, 1)

            def mask(i, r, tiles):
                if tiles[0] == 0:
                    dve.wait_ge(s_exp, EX_N * (i + 1))
                    ahead(dve, s_tr, TR_N * i, i - 1 if known(i) else i)
                for t in tiles:
                    dve.scalar_tensor_tensor(PR[:, t, :], S[r % 2][:, t, :], TV[:, t:t + 1], E[r % 2][:, t, :],
                                             ALU.is_ge, ALU.mult).then_inc(s_prob, 1)

            def back_ctx(b, r):
                seen = step(s_bd, BD, b)
                dve.wait_ge(s_bp, BP * b + 2)
                dve.reciprocal(RD[:, :, :], chunks(bY, KC, T)).then_inc(s_bd, 1)
                seen(1)
                dve.tensor_tensor(CT[:, :, :], chunks(bX, KC, T), RD[:, :, :], ALU.mult).then_inc(s_bd, 1)

            def back_res(b, r):
                seen = step(s_bd, BD, b)
                dve.wait_ge(s_bp, BP * b + 3)
                dve.tensor_tensor(HM[:, :, :], chunks(bX, 2, D), H[r][:, :, :], ALU.add).then_inc(s_bd, 1)
                seen(3)
                dve.bn_stats(bst[:, 0, :], HM[:, 0, :]).then_inc(s_bd, 1)
                dve.bn_stats(bst[:, 1, :], HM[:, 1, :]).then_inc(s_bd, 1)
                seen(5)
                gated()
                dve.bn_aggr(bmv[:, 0, :], bst[:, 0, :]).then_inc(s_bd, 1)
                dve.bn_aggr(bmv[:, 1, :], bst[:, 1, :]).then_inc(s_bd, 1)

            def back_norm(b, r):
                dve.wait_ge(s_bg, BG * b + 2)
                ahead(dve, s_xrow[r % 2], of_ring(b - 2, r % 2, 2, 32), b - 2 if known(b) else b)
                for c in range(2):
                    dve.tensor_scalar(X2[r % 2][:, c, 0:D], HM[:, c, :], bmv[:, c, 0:1], brs[:, c:c + 1],
                                      ALU.subtract, ALU.mult).then_inc(s_bd, 1)

            def back_glu(b):
                seen = step(s_bd, BD, b)
                dve.wait_ge(s_ba, BA * b + 2)
                g, u = chunks(bX, NF, T)[0:FC], chunks(bY, NF, T)[0:FC]
                dve.scalar_tensor_tensor(TH[:, :, :], TH[:, :, :], 1.0, g, ALU.add, ALU.mult).then_inc(s_bd, 1)
                seen(10)
                dve.wait_ge(s_bp, BP * b + 6)
                dve.scalar_tensor_tensor(HT[:, :, :], TH[:, :, :], 0.5, u, ALU.mult, ALU.mult).then_inc(s_bd, 1)

            def back_out(b, r):
                ahead(dve, s_out[r % 2], of_ring(b - 2, r % 2, 2, 32), b - 2 if known(b) else b)
                dve.wait_ge(s_bp, BP * b + 7)
                dve.tensor_tensor(OT[r % 2][:, :, :], chunks(bX, 2, D), HM[:, :, :], ALU.add).then_inc(s_bd, 1)

            def back_top(b):
                seen = step(s_bd, BD, b)
                dve.wait_ge(s_bp, BP * b + 8)
                gated()
                for c in range(2):
                    dve.max(L8[:, c, :], chunks(bY, 2, NE)[:, c, :]).then_inc(s_bd, 1)
                seen(14)
                gated()
                for c in range(2):
                    dve.match_replace(MR[:, c, :], L8[:, c, :], chunks(bY, 2, NE)[:, c, :], LOW).then_inc(s_bd, 1)
                seen(16)
                dve.scalar_tensor_tensor(MK[:, :, :], MR[:, :, :], GONE, PAD[:, :, :], ALU.is_lt, ALU.mult).then_inc(s_bd, 1)

            def back_weights(b, r):
                seen = step(s_bd, BD, b)
                dve.wait_ge(s_ba, BA * b + 7)
                dve.reciprocal(r8[:, :], s8[:, :]).then_inc(s_bd, 1)
                seen(18)
                for c in range(2):
                    dve.tensor_scalar(X2[r % 2][:, c, D:XW], EX[:, c, :], r8[:, c:c + 1], None, ALU.mult).then_inc(s_bd, 1)

            def back_slots(b, r):
                seen = step(s_bd, BD, b)
                dve.wait_ge(s_bp, BP * b + 9)
                cum = bY[:, 2 * NE:5 * NE].rearrange("p (c n) -> p c n", c=3)
                cb = carry[:, :].rearrange("p (a n) -> p a n", a=1).to_broadcast([P, 2, NE])
                dve.tensor_tensor(PO[:, :, :], cum[:, 0:2, :], cb, ALU.add).then_inc(s_bd, 1)
                seen(21)
                dve.tensor_tensor(carry[:, :], cum[:, 2, :], carry[:, :], ALU.add).then_inc(s_bd, 1)
                dve.scalar_tensor_tensor(KEEP[:, :, :], PO[:, :, :], float(CAP), MK[:, :, :], ALU.is_lt, ALU.mult).then_inc(s_bd, 1)
                for c in range(2):
                    last = dve.scalar_tensor_tensor(MR[:, c, :], PO[:, c, :], -1.0, CST[:, :], ALU.mult, ALU.add)
                last.then_inc(s_bd, 1)
                seen(24)
                dve.tensor_tensor(MR[:, :, :], MR[:, :, :], KEEP[:, :, :], ALU.mult).then_inc(s_bd, 1)
                seen(25)
                gated()
                for c in range(2):
                    dve.max(N8[:, c, :], MR[:, c, :]).then_inc(s_bd, 1)
                ahead(dve, s_slot[r % 2], of_ring(b - 2, r % 2, 2, SL), b - 2 if known(b) else b)
                seen(27)
                dve.tensor_scalar(SLOT[r % 2][:, :, :], N8[:, :, :], -1.0, float(FAR), ALU.mult, ALU.add).then_inc(s_bd, 1)

            def iteration(i, r):
                f, b, o = has(i + 1), has(i - 2), has(i - 3)
                rf, rb, ro = (r + 1) % RING, (r - 2) % RING, (r - 3) % RING
                for n in range(NT + 3):
                    if has(i) and n % 2 == 0 and n // 2 < NG:
                        take(i, r, n // 2)
                    if has(i - 1):
                        pick(i - 1, (r - 1) % RING, n)
                    if f and n == 2:
                        front_embed(i + 1)
                    if o and n == 5:
                        back_glu(i - 3)
                    if f and n == 6:
                        front_embed2(i + 1)
                    if f and n == 8:
                        front_norm(i + 1, rf)
                    if o and n == 9:
                        back_out(i - 3, ro)
                        back_top(i - 3)
                    if f and n == 11:
                        front_norm2(i + 1, rf)
                    if o and n == 14:
                        back_weights(i - 3, ro)
                    if o and n == 15:
                        back_slots(i - 3, ro)
                if b:
                    back_ctx(i - 2, rb)
                if has(i - 1):
                    threshold(i - 1)
                if b:
                    back_res(i - 2, rb)
                if has(i - 1):
                    general(i - 1, (r - 1) % RING)
                    mask(i - 1, (r - 1) % RING, range(0, NT // 2))
                if b:
                    back_norm(i - 2, rb)
                if has(i - 1):
                    mask(i - 1, (r - 1) % RING, range(NT // 2, NT))

            batches(dve, iteration)

            dve.wait_ge(s_ids, 16)
            dve.tensor_copy(ids_f[:, :], ids_i[:, :]).then_inc(s_idt, 1)
            dve.wait_ge(s_idp, 1)
            dve.tensor_copy(ids_t[:, :], bI[:, 0:NE]).then_inc(s_idt, 1)
            dve.wait_ge(s_idt, 2)

            def index(e, k):
                ahead(dve, s_add, 16 * (e - EB + 1), e - EB if known(e) else e)
                dve.tensor_copy(IX[k][:, :], ids_t[:, bass.ds(e, 1)]).then_inc(s_ix, 1)

            def expert(e, k):
                g, u = chunks(bX, NF, P)[0:FC], chunks(bY, NF, P)[0:FC]
                dve.wait_ge(s_ea, 2 * e + 2)
                dve.scalar_tensor_tensor(TG[:, :, :], TE[:, :, :], 1.0, g, ALU.add, ALU.mult).then_inc(s_ed, 1)
                dve.wait_ge(s_ep, 4 * e + 3)
                dve.wait_ge(s_ed, 3 * e + 1)
                dve.scalar_tensor_tensor(HE[:, :, :], TG[:, :, :], 0.5, u, ALU.mult, ALU.mult).then_inc(s_ed, 1)
                dve.wait_ge(s_ep, 4 * e + 4)
                dve.tensor_scalar(Y[k][:, :], bF[:, 0:D], XG[k][:, bass.ds(e + D, 1)], None, ALU.mult).then_inc(s_ed, 1)

            def both(e, k):
                expert(e, k)
                if not known(e) or e + 2 < NE:
                    index(e + 2, (k + 2) % EB)

            index(0, 0)
            index(1, 1)
            experts(dve, both)

        @block.tensor
        def _(pe):
            pe.wait_ge(s_bo, 2)
            for k in range(KC):
                last = pe.matmul(bX[:, 0:D], BVR[:, k, :], WO[:, k, :], start=(k == 0), stop=(k == KC - 1))
            last.then_inc(s_bv, 1)
            pe.wait_ge(s_setup, 3)

            def front_embed(b, r):
                pe.wait_ge(s_patch[r % 2], of_ring(b, r % 2, 2, 16))
                ahead(pe, s_fa, FA * b, b - 1 if known(b) else b)
                for k in range(PK):
                    last = pe.matmul(bF[0:IMG, 0:D], PT[r % 2][:, k, :], WT[:, k, :], start=(k == 0), stop=(k == PK - 1))
                last.then_inc(s_fp, 1)

            def front_xt(b):
                pe.wait_ge(s_fd, FD * b + 9)
                for c in range(2):
                    n, lo, hi = parts(c)
                    for k in range(KC):
                        last = pe.transpose(chunks(bF, KC, T)[:, k, lo:hi], XN[0:n, c, P * k:P * k + P], IDENT[0:n, 0:n])
                last.then_inc(s_fp, 1)

            def front_qk(b, which):
                pe.wait_ge(s_fa, FA * b + (1 if which == 0 else 3))
                for m in range(KC):
                    for k in range(KC):
                        at = D * which + P * m
                        last = pe.matmul(chunks(bF, KC, T)[:, m, :], WQ[:, k, at:at + P], XT[:, k, :],
                                         start=(k == 0), stop=(k == KC - 1))
                last.then_inc(s_fp, 1)

            def front_v(b):
                pe.wait_ge(s_fa, FA * b + 5)
                for c in range(2):
                    n, lo, hi = parts(c)
                    for k in range(KC):
                        last = pe.matmul(chunks(bF, 2, D)[0:n, c, :], XT[:, k, lo:hi], WQ[:, k, 2 * D:3 * D],
                                         start=(k == 0), stop=(k == KC - 1))
                last.then_inc(s_fp, 1)

            def scores(i, g):
                if g == 0:
                    pe.wait_ge(s_diag, DG * (i + 1))
                    pe.wait_ge(s_fg, FG * (i + 1))
                if g >= 3:
                    pe.wait_ge(s_take, NT * i + GROUP * (g - 2))
                    pe.wait_ge(s_exp, EX_N * i + (2 * GROUP + 1) * (g - 2))
                elif g == 0:
                    ahead(pe, s_take, NT * i, i - 1 if known(i) else i)
                    ahead(pe, s_exp, EX_N * i, i - 1 if known(i) else i)
                for t in range(GROUP * g, GROUP * (g + 1)):
                    o = chunks(bS[g % 3], GROUP, T)[:, t % GROUP, :]
                    if t <= MIXED:
                        last = pe.matmul(o, QA[:, P * t:P * t + P], KZ[:, 0, :], start=True, stop=(t < MIXED))
                    if t >= MIXED:
                        at = P * (t - MIXED)
                        last = pe.matmul(o, QB[:, at:at + P], KZ[:, 1, :], start=(t > MIXED), stop=True)
                last.then_inc(s_score, 1)

            def transposes(i, n):
                for t in range(4 * n, min(4 * n + 4, NT)):
                    pe.wait_ge(s_prob, NT * i + t + 1)
                    if t % 4 == 0:
                        ahead(pe, s_trc, TRC_N * i + 2 * n, i if n else (i - 1 if known(i) else i))
                    at = P * (t % 4)
                    pe.transpose(bT[:, at:at + P], PR[:, t, IMG:T], IDENT[:, :])
                    pe.transpose(bI[0:IMG, at:at + P], PR[:, t, 0:IMG], IDENT[:, :]).then_inc(s_tr, 1)

            def sure(i):
                pe.wait_ge(s_sel, SEL * i + 8)
                pe.matmul(bT[0:1, 0:1], okc[:, :], ONES[:, 0:1], start=True, stop=True).then_inc(s_flag, 1)

            def context(i, r):
                pe.wait_ge(s_trc, TRC_N * (i + 1))
                ahead(pe, s_bd, BD * i, i - 1 if known(i) else i)
                for out_b, what in ((bX, "values"), (bY, "sums")):
                    for hf in range(KC):
                        o = chunks(out_b, KC, T)[:, hf, :]
                        for n, (a, c) in enumerate(((0, 0), (0, 1), (1, 0), (1, 1))):
                            for g in range(4):
                                h = HALF * hf + 2 * g + a
                                p = (PTT, PTI)[c][:, T * h:T * h + T]
                                w = VZ[r][:, c, 2 * HD * h:2 * HD * (h + 1)] if what == "values" else ONESZ[:, a, :]
                                last = pe.matmul(o[2 * HD * g:2 * HD * (g + 1)], w, p, start=(n == 0), stop=(n == 3),
                                                 skip_group_check=True)
                    last.then_inc(s_bp, 1)

            def back_proj(b):
                pe.wait_ge(s_bd, BD * b + 2)
                for c in range(2):
                    lo = IMG if c == 0 else 0
                    for k in range(KC):
                        last = pe.matmul(chunks(bX, 2, D)[:, c, :], CT[:, k, lo:lo + P], WO[:, k, :],
                                         start=(k == 0), stop=(k == KC - 1))
                last.then_inc(s_bp, 1)

            def back_xt(b, r):
                pe.wait_ge(s_bd, BD * b + 9)
                for c in range(2):
                    n, lo, hi = parts(c)
                    for k in range(KC):
                        last = pe.transpose(chunks(bY, KC, T)[:, k, lo:hi], X2[r % 2][0:n, c, P * k:P * k + P], IDENT[0:n, 0:n])
                last.then_inc(s_bp, 1)

            def back_glu(b):
                pe.wait_ge(s_ba, BA * b + 1)
                for n, bank in enumerate((bX, bY)):
                    for f in range(NF):
                        for k in range(KC):
                            at = FF * n + FC * f
                            last = pe.matmul(chunks(bank, NF, T)[0:FC, f, :], WSG[:, k, at:at + FC], X2T[:, k, :],
                                             start=(k == 0), stop=(k == KC - 1))
                    last.then_inc(s_bp, 1)

            def back_down(b):
                pe.wait_ge(s_bd, BD * b + 11)
                for c in range(2):
                    lo = IMG if c == 0 else 0
                    for f in range(NF):
                        last = pe.matmul(chunks(bX, 2, D)[:, c, :], HT[:, f, lo:lo + P], WSD[:, f, :],
                                         start=(f == 0), stop=(f == NF - 1))
                last.then_inc(s_bp, 1)
                for c in range(2):
                    lo = IMG if c == 0 else 0
                    for k in range(KC):
                        last = pe.matmul(chunks(bY, 2, NE)[:, c, :], X2T[:, k, lo:lo + P], WR[:, k, :],
                                         start=(k == 0), stop=(k == KC - 1))
                last.then_inc(s_bp, 1)

            def back_count(b):
                pe.wait_ge(s_bd, BD * b + 17)
                pe.wait_ge(s_ba, BA * b + 5)
                cum = bY[:, 2 * NE:5 * NE].rearrange("p (c n) -> p c n", c=3)
                pe.matmul(cum[:, 0, :], TRI[:, :], MK[:, 0, :], start=True, stop=False)
                pe.matmul(cum[:, 0, :], ONES[:, :], MK[:, 1, :], start=False, stop=True)
                pe.matmul(cum[:, 1, :], TRI[:, :], MK[:, 1, :], start=True, stop=True)
                pe.matmul(cum[:, 2, :], ONES[:, :], MK[:, 0, :], start=True, stop=False)
                pe.matmul(cum[:, 2, :], ONES[:, :], MK[:, 1, :], start=False, stop=True).then_inc(s_bp, 1)

            def iteration(i, r):
                f, b, o = has(i + 1), has(i - 2), has(i - 3)
                rf, rb = (r + 1) % RING, (r - 2) % RING
                for g in range(NG):
                    if has(i):
                        scores(i, g)
                    if f and g == 0:
                        front_embed(i + 1, rf)
                    if b and g < TRC_N // 2:
                        transposes(i - 2, g)
                    if o and g == 1:
                        back_glu(i - 3)
                    if o and g == 3:
                        back_down(i - 3)
                if o:
                    back_count(i - 3)
                if f:
                    front_xt(i + 1)
                    front_qk(i + 1, 0)
                if b:
                    context(i - 2, rb)
                if f:
                    front_qk(i + 1, 1)
                if b:
                    back_proj(i - 2)
                if f:
                    front_v(i + 1)
                if has(i - 1):
                    sure(i - 1)
                if b:
                    back_xt(i - 2, rb)

            batches(pe, iteration)

            pe.wait_ge(s_idt, 1)
            pe.transpose(bI[:, 0:NE], ids_f[:, :], IDENT[0:NE, 0:NE]).then_inc(s_idp, 1)

            def expert(e, k):
                pe.wait_ge(s_xg[k], of_ring(e, k, EB, 16))
                for c in range(KC):
                    last = pe.transpose(chunks(bT, KC, P)[:, c, :], XG[k][:, P * c:P * c + P], IDENT[:, :])
                last.then_inc(s_ep, 1)
                pe.wait_ge(s_ea, 2 * e + 1)
                pe.wait_ge(s_ew[k], of_ring(e, k, EB, 48))
                for n, (bank, w) in enumerate(((bX, WG[k]), (bY, WU[k]))):
                    for f in range(NF):
                        for c in range(KC):
                            last = pe.matmul(chunks(bank, NF, P)[0:FC, f, :], w[:, c, FC * f:FC * f + FC], XE[:, c, :],
                                             start=(c == 0), stop=(c == KC - 1))
                    last.then_inc(s_ep, 1)
                pe.wait_ge(s_ed, 3 * e + 2)
                for f in range(NF):
                    last = pe.matmul(bF[:, 0:D], HE[:, f, :], WD[k][:, f, :], start=(f == 0), stop=(f == NF - 1))
                last.then_inc(s_ep, 1)

            experts(pe, expert)


def kernel(x, txt, L0_tok_W, L0_tok_b, L0_tok_cls_token, L0_tok_pos_embedding, L0_tok_gamma, L0_tok_beta,
           L0_attn_W_qkv, L0_attn_b_qkv, L0_attn_W_out, L0_attn_b_out, L0_ffn_router_w, L0_ffn_w_gate, L0_ffn_w_up,
           L0_ffn_w_down, L0_ffn_ws_gate_up, L0_ffn_ws_down):
    import numpy as np
    import concourse.bacc as bacc
    from concourse.bass_utils import run_bass_kernel_spmd

    n_batch = x.shape[0]
    patches = np.asarray(x).reshape(n_batch, 3, 6, 16, 6, 16).transpose(0, 1, 3, 5, 2, 4).reshape(n_batch, PK, P, IMG - 1)
    bq, bk, bv = (np.asarray(L0_attn_b_qkv)[D * n:D * (n + 1)].reshape(KC, P).T for n in range(3))
    named = dict(patches=patches.transpose(0, 2, 1, 3), txt=txt, w_tok=L0_tok_W, b_tok=L0_tok_b, cls=L0_tok_cls_token,
                 pos=L0_tok_pos_embedding, gamma=L0_tok_gamma, beta=L0_tok_beta, w_qkv=np.asarray(L0_attn_W_qkv).T,
                 b_q=bq, b_k=bk, b_v=bv, w_out=np.asarray(L0_attn_W_out).T, b_out=L0_attn_b_out,
                 router=np.asarray(L0_ffn_router_w).T, w_gate=L0_ffn_w_gate, w_up=L0_ffn_w_up, w_down=L0_ffn_w_down,
                 ws_gate_up=L0_ffn_ws_gate_up, ws_down=L0_ffn_ws_down)
    nc = bacc.Bacc("TRN2", target_bir_lowering=False, num_devices=1)
    arrays = {f"in_{k}": np.ascontiguousarray(v) for k, v in named.items()}
    args = {k: nc.dram_tensor(f"in_{k}", arrays[f"in_{k}"].shape, fp32, kind="ExternalInput").ap() for k in named}
    out = nc.dram_tensor("out", (n_batch * T + CAP, D), fp32, kind="ExternalOutput").ap()
    early_fusion_kernel(nc, *args.values(), out, n_batch)
    r = run_bass_kernel_spmd(nc, [arrays], core_ids=[0])
    return r.results[0]["out"][0:n_batch * T].reshape(n_batch, T, D)
```
